# Optimizing a Trainium2 kernel written in Bass

```python
import numpy as np
import jax
import jax.numpy as jnp

def _softmax(x, axis=-1):
    return jax.nn.softmax(x, axis=axis)

def _gelu(x):
    return jax.nn.gelu(x, approximate=True)

def _silu(x):
    return jax.nn.silu(x)

def _sigmoid(x):
    return jax.nn.sigmoid(x)

def _layernorm(x, axis=-1, eps=1e-05):
    m = jnp.mean(x, axis=axis, keepdims=True)
    v = jnp.var(x, axis=axis, keepdims=True)
    return (x - m) / jnp.sqrt(v + eps)

def _scatter_add(tgt, idx, src, axis=0):
    return tgt.at[idx].add(src)

def _segment_sum(src, seg, n):
    return jax.ops.segment_sum(src, seg, n)
kernel_name = 'mk_prb_d1_jaxref_r4_65530d'

def setup_inputs(seed: int=0):
    np.random.seed(seed)
    _w = jnp.asarray

    def _L0_attn_setup():
        import jax, jax.numpy as jnp
        import numpy as np
        B, S, D_MODEL, N_HEADS = (2, 512, 512, 16)
        HEAD_DIM = D_MODEL // N_HEADS
        ROPE_BASE = 10000.0

        def _rope_cos_sin(seq_len, head_dim, dtype):
            inv_freq = 1.0 / ROPE_BASE ** (jnp.arange(0, head_dim, 2, dtype=jnp.float32) / head_dim)
            t = jnp.arange(seq_len, dtype=jnp.float32)
            freqs = jnp.outer(t, inv_freq)
            emb = jnp.concatenate([freqs, freqs], axis=-1)
            return (jnp.cos(emb).astype(dtype), jnp.sin(emb).astype(dtype))

        def _rotate_half(x):
            half = x.shape[-1] // 2
            return jnp.concatenate([-x[..., half:], x[..., :half]], axis=-1)

        def _apply_rope(q, k):
            cos, sin = _rope_cos_sin(q.shape[2], q.shape[3], q.dtype)
            cos = cos[None, None]
            sin = sin[None, None]
            q = q * cos + _rotate_half(q) * sin
            k = k * cos + _rotate_half(k) * sin
            return (q, k)
        key = jax.random.key(seed)
        kx, kq, kk, kv, ko = jax.random.split(key, 5)
        s = 1.0 / np.sqrt(D_MODEL)
        return {'x': jax.random.normal(kx, (B, S, D_MODEL), dtype=jnp.float32), 'Wq': jax.random.normal(kq, (D_MODEL, D_MODEL), dtype=jnp.float32) * s, 'Wk': jax.random.normal(kk, (D_MODEL, D_MODEL), dtype=jnp.float32) * s, 'Wv': jax.random.normal(kv, (D_MODEL, D_MODEL), dtype=jnp.float32) * s, 'Wo': jax.random.normal(ko, (D_MODEL, D_MODEL), dtype=jnp.float32) * s}
    _L0_attn_in = _L0_attn_setup()

    def _L0_ffn_setup():
        import jax, jax.numpy as jnp
        import numpy as np
        NUM_EXPERTS_PER_TOK = 2
        key = jax.random.key(seed)
        k1, k2, k3, k4 = jax.random.split(key, 4)
        B, S, D, O, E = (4, 512, 512, 512, 8)
        x = jax.random.normal(k1, (B, S, D), dtype=jnp.float32)
        gate_w = jax.random.normal(k2, (E, D), dtype=jnp.float32) * (1.0 / np.sqrt(D))
        expert_w = jax.random.normal(k3, (E, O, D), dtype=jnp.float32) * (1.0 / np.sqrt(D))
        expert_b = jax.random.normal(k4, (E, O), dtype=jnp.float32) * 0.01
        return {'x': x, 'gate_w': gate_w, 'expert_w': expert_w, 'expert_b': expert_b}
    _L0_ffn_in = _L0_ffn_setup()
    _d = {'L0_attn_x': _L0_attn_in['x'], 'L0_attn_Wq': _L0_attn_in['Wq'], 'L0_attn_Wk': _L0_attn_in['Wk'], 'L0_attn_Wv': _L0_attn_in['Wv'], 'L0_attn_Wo': _L0_attn_in['Wo'], 'L0_ffn_gate_w': _L0_ffn_in['gate_w'], 'L0_ffn_expert_w': _L0_ffn_in['expert_w'], 'L0_ffn_expert_b': _L0_ffn_in['expert_b']}
    _x0 = _d['L0_attn_x']
    _d['L0_attn_x'] = jax.random.normal(jax.random.fold_in(jax.random.key(seed), 1), (8, 512, 512), dtype=_x0.dtype)
    del _x0
    return _d

def reference(L0_attn_x, L0_attn_Wq, L0_attn_Wk, L0_attn_Wv, L0_attn_Wo, L0_ffn_gate_w, L0_ffn_expert_w, L0_ffn_expert_b):

    def _L0_attn_ref(x, Wq, Wk, Wv, Wo):
        import jax, jax.numpy as jnp
        import numpy as np
        B, S, D_MODEL, N_HEADS = (2, 512, 512, 16)
        HEAD_DIM = D_MODEL // N_HEADS
        ROPE_BASE = 10000.0

        def _rope_cos_sin(seq_len, head_dim, dtype):
            inv_freq = 1.0 / ROPE_BASE ** (jnp.arange(0, head_dim, 2, dtype=jnp.float32) / head_dim)
            t = jnp.arange(seq_len, dtype=jnp.float32)
            freqs = jnp.outer(t, inv_freq)
            emb = jnp.concatenate([freqs, freqs], axis=-1)
            return (jnp.cos(emb).astype(dtype), jnp.sin(emb).astype(dtype))

        def _rotate_half(x):
            half = x.shape[-1] // 2
            return jnp.concatenate([-x[..., half:], x[..., :half]], axis=-1)

        def _apply_rope(q, k):
            cos, sin = _rope_cos_sin(q.shape[2], q.shape[3], q.dtype)
            cos = cos[None, None]
            sin = sin[None, None]
            q = q * cos + _rotate_half(q) * sin
            k = k * cos + _rotate_half(k) * sin
            return (q, k)
        bsz, seq_len, _ = x.shape

        def proj(W):
            return (x @ W.T).reshape(bsz, seq_len, N_HEADS, HEAD_DIM).transpose(0, 2, 1, 3)
        q, k, v = (proj(Wq), proj(Wk), proj(Wv))
        q, k = _apply_rope(q, k)
        scores = jnp.einsum('bhqd,bhkd->bhqk', q, k) / jnp.sqrt(jnp.float32(HEAD_DIM)).astype(x.dtype)
        causal = jnp.tril(jnp.ones((seq_len, seq_len), dtype=bool))
        scores = jnp.where(causal[None, None], scores, jnp.finfo(scores.dtype).min)
        attn = jax.nn.softmax(scores, axis=-1)
        out = jnp.einsum('bhqk,bhkd->bhqd', attn, v)
        out = out.transpose(0, 2, 1, 3).reshape(bsz, seq_len, D_MODEL)
        return out @ Wo.T

    def _L0_ffn_ref(x, gate_w, expert_w, expert_b):
        import jax, jax.numpy as jnp
        import numpy as np
        NUM_EXPERTS_PER_TOK = 2
        B, S, D = x.shape
        xf = x.reshape(B * S, D)
        gate_logits = xf @ gate_w.T
        top_vals, top_idx = jax.lax.top_k(gate_logits, NUM_EXPERTS_PER_TOK)
        w = jax.nn.softmax(top_vals.astype(jnp.float32), axis=-1).astype(x.dtype)
        y_all = jnp.einsum('td,eod->teo', xf, expert_w) + expert_b[None, :, :]
        y_sel = jnp.take_along_axis(y_all, top_idx[:, :, None], axis=1)
        out = jnp.sum(y_sel * w[:, :, None], axis=1)
        return out.reshape(B, S, -1)
    x = L0_attn_x
    xn = _layernorm(x, axis=-1)
    x = x + _L0_attn_ref(xn, L0_attn_Wq, L0_attn_Wk, L0_attn_Wv, L0_attn_Wo) + _L0_ffn_ref(xn, L0_ffn_gate_w, L0_ffn_expert_w, L0_ffn_expert_b)
    return x

_drawn_inputs = setup_inputs


def setup_inputs(seed=0):
    import zlib

    import numpy as np

    out = dict(_drawn_inputs(seed))
    spreads = {}
    factors = {'L0_ffn_expert_b': 8.0}
    for name, (base, spread) in spreads.items():
        noise = np.random.default_rng([zlib.crc32(name.encode()), seed]).standard_normal(out[name].shape)
        drawn = base * np.exp(spread * noise) if base else spread * noise
        out[name] = jnp.asarray(drawn.astype(out[name].dtype))
    for name, factor in factors.items():
        out[name] = (out[name] * factor).astype(out[name].dtype)
    return out
```

```python
import numpy as np

import concourse.bass as bass
from concourse import mybir

F32 = mybir.dt.float32
F16 = mybir.dt.float16
BF16 = mybir.dt.bfloat16
I32 = mybir.dt.int32
ALU = mybir.AluOpType
ACT = mybir.ActivationFunctionType
AX = mybir.AxisListType

P = 128
EXP_ONE = 1 << 23
EPS = 1e-5
LOG_X = 11
LOG_W = 14
LOG_V = 20
MASKED = -3.0e38


class Steps:

    def __init__(self, engine, sem):
        self.engine, self.sem, self.n, self.before = engine, sem, 0, 0

    def link(self, ins, wait=None):
        self.n += 1
        ins.then_inc(self.sem, 1)
        (wait or type(self.engine).wait_ge)(self.engine, self.sem, self.before + self.n)

    def enter(self, per_turn):
        self.outside, self.per_turn = self.n, per_turn

    def turn(self, i):
        self.n, self.before = 0, self.outside + i * self.per_turn

    def leave(self, turns):
        assert self.n == self.per_turn, (self.n, self.per_turn)
        self.n, self.before = self.outside + turns * self.per_turn, 0


def moe_attention_layer(nc, x, w_all, gate, bias, trig, small, out):
    B, S, D = x.shape
    NM = w_all.shape[0]
    E = gate.shape[2]
    NQ = NM - E
    C = D // P
    J = S // P
    T = B * S
    NT = T // P
    NTILE = -(-(2 * NT + E - 1) // 4) * 4
    NCOL = E * NT + 8
    HG = 4
    G = D // P
    HD = P // HG
    N = B * G
    x_v = x.rearrange("b (j p) d -> b p j d", p=P)
    x_t = x.rearrange("b (j p) d -> (b j) p d", p=P)
    out_t = out.rearrange("b (j p) d -> (b j) p d", p=P)

    xn_rows = nc.dram_tensor("xn_rows", (T, 2 * D), F16, kind="Internal").ap()
    slot_table = nc.dram_tensor("slot_table", (P * NCOL, 1), I32, kind="Internal").ap()
    y_rows = nc.dram_tensor("y_rows", (NTILE * P, D), F32, kind="Internal").ap()

    place = [nc.sbuf_base + 127 & ~127]

    def at(name, shape, dtype, offset=None):
        size = int(np.prod(shape[1:])) * (2 if dtype in (F16, BF16) else 4)
        o = place[0] if offset is None else offset
        t = nc.alloc_sbuf_tensor_at(name, shape, dtype, offset=o)
        place[0] = o + (size + 31 & ~31)
        return t

    ident16 = at("ident16", [P, P], F16)
    before16 = at("before16", [P, P], F16)
    ones16 = at("ones16", [P, P], F16)
    ident32 = at("ident32", [P, P], F32)
    causal = at("causal", [P, P], BF16)
    small_sb = at("small_sb", [P, small.shape[1]], F32)
    prefer = small_sb[:, 0:J * E].rearrange("p (j e) -> p j e", j=J)
    first_row = small_sb[:, J * E:J * E + E]
    tile_no = small_sb[:, J * E + E:J * E + E + NTILE]
    slots = at("slots", [P, 2, NT], I32)
    gap = at("gap", [P, NT], F32)
    w12 = at("w12", [P, 2, NT], F32)
    amax = at("amax", [P, 16], F32)
    amax_all = at("amax_all", [P, 16], F32)
    expo = at("expo", [P, 16], I32)
    up = at("up", [P, 16], I32)
    down = at("down", [P, 16], I32)
    factors = at("factors", [P, 3], F32)
    gate_hl = at("gate_hl", [P, C, 2 * E], F16)
    gate_f = at("gate_f", [P, C, E], F32)
    carry = at("carry", [P, E], F32)
    token_no = [at(f"token_no{u}", [P, J], I32) for u in range(2)]
    target = [at(f"target{u}", [P, 2, J], I32) for u in range(2)]
    xT = at("xT", [P, 2 * C, T], F16)
    end_common = place[0]
    w_exp = at("w_exp", [P, E, 2, C, D], F16)
    after_exp = place[0]

    x_in = [at(f"x_in{u}", [P, J, D], F32) for u in range(2)]
    x_n = at("x_n", [P, J, D], F32)
    x_hl = [at(f"x_hl{u}", [P, J, 2, D], F16) for u in range(2)]
    w_in = [at(f"w_in{u}", [P, C, D], F32) for u in range(2)]
    zero_i = at("zero_i", [P, NCOL], I32)
    stats = at("stats", [P, J, 6], F32)
    mean_var = at("mean_var", [P, J, 2], F32)
    var_eps = at("var_eps", [P, J], F32)
    std = at("std", [P, J], F32)
    r0 = at("r0", [P, J], F32)
    r1 = at("r1", [P, J], F32)
    rstd = at("rstd", [P, J], F32)
    logit = at("logit", [P, J, E], F32)
    rest = at("rest", [P, J, E], F32)
    best = at("best", [P, 2, J], F32)
    same = at("same", [P, J, E], F32)
    rank = at("rank", [P, J], F32)
    one_hot = [at(f"one_hot{k}", [P, J, E], F32) for k in range(2)]
    chosen = at("chosen", [P, J * E], F16)
    place_f = at("place_f", [P, J, E], F32)
    picked = at("picked", [P, 2, J, E], F32)
    slot_f = at("slot_f", [P, 2, J], F32)
    low7 = at("low7", [P, 2, J], I32)
    high = at("high", [P, 2, J], I32)

    place[0] = after_exp
    w_att = at("w_att", [P, NQ, 2, C, D], F16)
    bias_all = at("bias_all", [P, E, D], F32)
    moe0 = place[0]
    wq_in = [at(f"wq_in{u}", [P, C, D], F32) for u in range(2)]
    place[0] = moe0
    x_g = [at(f"x_g{u}", [P, 2 * D], F16) for u in range(4)]
    x_gT = [at(f"x_gT{u}", [P, 2 * C, P], F16) for u in range(2)]
    y_sb = [at(f"y_sb{u}", [P, D], F32) for u in range(4)]
    idx = [at(f"idx{u}", [P, 1], I32) for u in range(4)]
    tok_of = at("tok_of", [P, NCOL], I32)
    slot_e = at("slot_e", [P, 2, NT], F32)
    slot_i = at("slot_i", [P, 2, NT], I32)
    slot_now = at("slot_now", [P, 2, NT], F32)
    move = at("move", [P, 2, NT], F32)
    moves = at("moves", [P, E], F32)
    exp_col = at("exp_col", [P, 2, NTILE], I32)
    cnt_i = at("cnt_i", [P, E], I32)
    tiles = at("tiles", [P, E], F32)
    ends = at("ends", [P, 2, E], F32)
    past = at("past", [P, NTILE, E], F32)
    n_past = at("n_past", [P, NTILE], F32)
    t_past = at("t_past", [P, NTILE], F32)
    t_col = at("t_col", [P, NTILE], F32)

    place[0] = end_common
    pT = at("pT", [P, HG, J, S], F32)
    o_hl = at("o_hl", [P, G, 2, S], F16)
    q_stack = [at(f"q_stack{u}", [P, HG, S], F16) for u in range(2)]
    k_stack = [at(f"k_stack{u}", [P, HG, S], F16) for u in range(2)]
    assert place[0] <= after_exp
    place[0] = moe0 - 4 * E * D
    trig_sb = at("trig_sb", [P, 2, S], F32)
    plain = [at(f"plain_{n}", [P, S], F32) for n in "qk"]
    turned = [at(f"turned_{n}", [P, S], F32) for n in "qk"]
    qk_hl = [at(f"{n}_hl", [P, 2, S], F16) for n in "qk"]
    v_sb = [at(f"v_sb{u}", [P, J, P], F32) for u in range(2)]
    p_sb = [at(f"p_sb{u}", [P, 2, S], F32) for u in range(2)]
    o_sb = at("o_sb", [P, S], F32)
    sum_sb = [at(f"sum_sb{u}", [P, D], F32) for u in range(2)]
    y_in = [at(f"y_in{u}", [P, 2, D], F32) for u in range(2)]
    idx_y = [at(f"idx_y{u}", [P, 2], I32) for u in range(2)]
    top = at("top", [P, 2, 2], F32)
    shift = at("shift", [P, 2, 2], F32)
    den = [at(f"den{u}", [P, J, HG], F32) for u in range(2)]
    rden = at("rden", [P, J, HG, HD], F32)

    psum = nc.alloc_psum_tensor("psum", [P, 8, 512], F32)
    banks = [psum[:, i, :] for i in range(8)]

    def s_banks(u):
        return psum[:, BANK_S + 2 * u:BANK_S + 2 * u + 2, :]

    def half(bank):
        return banks[bank].bitcast(F16)

    def sem(name):
        return nc.alloc_semaphore(name)

    const_in, gate_in, table_zero = sem("const_in"), sem("gate_in"), sem("table_zero")
    x_loaded = [sem("x_loaded0"), sem("x_loaded1")]
    w_loaded = [sem("w_loaded0"), sem("w_loaded1")]
    xn_stored = [sem("xn_stored0"), sem("xn_stored1")]
    dve_own, pool_own = sem("dve_own"), sem("pool_own")
    consts_made = sem("consts_made")
    amax_done, amax_everywhere, scale_done = sem("amax_done"), sem("amax_everywhere"), sem("scale_done")
    w_hi_done, w_lo_done = sem("w_hi_done"), sem("w_lo_done")
    var_done, std_done, xn_done, x_hi_done, x_lo_done = (sem(n) for n in ("var_done", "std_done", "xn_done", "x_hi_done", "x_lo_done"))
    xt_done, xT_copied, gate_done, logit_read = (sem(n) for n in ("xt_done", "xT_copied", "gate_done", "logit_read"))
    chosen_done, rank_done, rank_read, target_done = (sem(n) for n in ("chosen_done", "rank_done", "rank_read", "target_done"))
    scattered = [sem("scattered0"), sem("scattered1")]
    gap_done, gap_exp, w12_done, tiles_done, table_loaded, bias_loaded = (sem(n) for n in ("gap_done", "gap_exp", "w12_done", "tiles_done", "table_loaded", "bias_loaded"))
    slots_final = sem("slots_final")
    gathered = [sem(f"gathered{u}") for u in range(4)]
    xg_turned, xgT_copied, y_done, y_scaled = (sem(n) for n in ("xg_turned", "xgT_copied", "y_done", "y_scaled"))
    y_stored = [sem(f"y_stored{u}") for u in range(4)]
    waited_apart = sem("waited_apart")
    trig_in, qk_summed, qk_rotated, qk_roped, qk_hi, qk_lo = (sem(n) for n in ("trig_in", "qk_summed", "qk_rotated", "qk_roped", "qk_hi", "qk_lo"))
    q_stacked = [sem(f"q_stacked{u}") for u in range(2)]
    k_stacked = [sem(f"k_stacked{u}") for u in range(2)]
    v_summed, v_read, factors_done = sem("v_summed"), sem("v_read"), sem("factors_done")
    scores_done, shift_done, exp_done, pt_turned = (sem(n) for n in ("scores_done", "shift_done", "exp_done", "pt_turned"))
    pt_copied = [sem(f"pt_copied{u}") for u in range(2)]
    rden_done, pv_done, o_read, o_hi, o_lo = (sem(n) for n in ("rden_done", "pv_done", "o_read", "o_hi", "o_lo"))
    wo_done, wo_read, sum_done = (sem(n) for n in ("wo_done", "wo_read", "sum_done"))
    x_again = [sem(f"x_again{u}") for u in range(2)]
    y_back = [sem(f"y_back{u}") for u in range(2)]
    out_stored = [sem(f"out_stored{u}") for u in range(2)]

    BANK_XT, BANK_GATE, BANK_RANK = 0, 4, 6

    def scale_ops(dve, own, m, at=None):
        own.link(dve.tensor_scalar(expo[:, m].bitcast(F32), amax_all[:, m if at is None else at], 2.0 ** -60, None, ALU.max))
        own.link(dve.tensor_scalar(expo[:, m], expo[:, m], 0x7F800000, None, ALU.bitwise_and))
        own.link(dve.tensor_scalar(up[:, m], expo[:, m], -1.0, float((254 + LOG_W) * EXP_ONE), ALU.mult, ALU.add))
        return dve.tensor_scalar(down[:, m], expo[:, m], float(-(LOG_W + LOG_X) * EXP_ONE), None, ALU.add)

    def wait_apart(engine, on, value):
        engine.wait_ge(on, value)
        engine.sem_inc(waited_apart, 1)

    GM = NM

    BANK_S, BANK_PT, BANK_MISC = 0, 4, 6
    BANK_Q, BANK_O = BANK_MISC, BANK_MISC + 1

    UNITS = 2 * J
    PT_FILLS = 13
    FILL_R = 2

    def fill(n, a):
        return PT_FILLS * n + a - 3

    def fills(k):
        return {7: (0, 1), 0: (3,), 1: (4,), 2: (5,), 3: (6,), 4: (7, 8), 5: (9, 10), 6: (11, 12)}[k]

    BY_ACT = (1, FILL_R, 6, 8, 10, 12)

    def pt_bank(g, a):
        return (PT_FILLS * g + a - 3) % 2

    def fills_up_to(bank, b, g, a):
        return b * (G * PT_FILLS // 2) + (PT_FILLS * g + a - 3 - bank) // 2 + 1

    def part(k, a):
        i, pair = k // 2, k % 2
        n = i + 1
        if len(fills(k)) == 1:
            return ([(2 * pair + h, j, (h * n + j) * P) for h in range(2) for j in range(n)],
                    lambda bank: bank[:, 0:2 * n * P].rearrange("p (h j t) -> p h j t", h=2, j=n),
                    pT[:, 2 * pair:2 * pair + 2, 0:n, i * P:(i + 1) * P])
        h = 2 * pair + fills(k).index(a)
        return ([(h, j, j * P) for j in range(n)],
                lambda bank: bank[:, 0:n * P].rearrange("p (j t) -> p j t", j=n),
                pT[:, h, 0:n, i * P:(i + 1) * P])

    block = nc.Block()
    with block:
        @block.sync
        def _(sp):
            sp.dma_start(small_sb[:], small).then_inc(const_in, 16)
            sp.dma_start(gate_f[:], gate).then_inc(gate_in, 16)

            def load(b, u, first=False):
                if not first:
                    sp.wait_ge(xn_done, b - 1)
                sp.dma_start(x_in[u][:], x_v[bass.ds(b, 1)].rearrange("b p j d -> p (b j) d")).then_inc(x_loaded[u], 16)
                if not first:
                    sp.wait_ge(w_lo_done, b)
                sp.dma_start(w_in[u][:], w_all[bass.ds(b, 1)].rearrange("b p c d -> p (b c) d")).then_inc(w_loaded[u], 16)

            def store(b, u):
                sp.wait_ge(x_hi_done, b + 1)
                sp.wait_ge(x_lo_done, b + 1)
                sp.dma_start(xn_rows[bass.ds(b * S, S), :].rearrange("(j p) c -> p j c", p=P),
                             x_hl[u][:].rearrange("p j h d -> p j (h d)")).then_inc(xn_stored[u], 16)

            load(0, 0, True)
            load(1, 1, True)
            sp.wait_ge(consts_made, 1)
            sp.dma_start(slot_table.rearrange("(p c) o -> p (c o)", p=P), zero_i[:]).then_inc(table_zero, 16)
            with sp.Fori(0, B // 2 - 1) as i:
                for u in range(2):
                    store(2 * i + u, u)
                    load(2 * i + 2 + u, u)
            for u in range(2):
                store(B - 2 + u, u)

            sp.wait_ge(w_lo_done, E + 1)
            sp.wait_ge(xt_done, NT)
            sp.wait_ge(target_done, B)
            for u in range(2):
                sp.wait_ge(xn_stored[u], 16 * (B // 2))
            sp.dma_start(bias_all[:], bias.unsqueeze(0).broadcast_to([P, E, D])).then_inc(bias_loaded, 16)
            for m in range(NQ):
                if m >= 2:
                    sp.wait_ge(w_lo_done, E + m)
                sp.dma_start(wq_in[m % 2][:], w_all[E + m]).then_inc(w_loaded[m % 2], 16)
            for u in range(2):
                sp.wait_ge(scattered[u], 16 * J * B)
            sp.dma_start(tok_of[:], slot_table.rearrange("(p c) o -> p (c o)", p=P)).then_inc(table_loaded, 16)
            sp.wait_ge(tiles_done, 1)

            def store_y(s, u):
                sp.wait_ge(y_scaled, s + 1)
                sp.dma_start(y_rows[bass.ds(s * P, P), :], y_sb[u][:]).then_inc(y_stored[u], 16)

            with sp.Fori(0, NTILE // 4) as i:
                for u in range(4):
                    store_y(4 * i + u, u)
            for u in range(4):
                sp.wait_ge(y_stored[u], 16 * (NTILE // 4))

            sp.wait_ge(y_scaled, NTILE)
            sp.dma_start(trig_sb[:], trig).then_inc(trig_in, 16)
            sp.wait_ge(y_done, NTILE)

            def stack(what, n, g, first):
                stacks, done, order = ((q_stack, q_stacked, (0, 1, 0, 1)), (k_stack, k_stacked, (0, 0, 1, 1)))[what]
                u = g % 2
                wait_apart(sp, qk_lo, 2 * n + what + 1)
                if not first:
                    sp.wait_ge(scores_done, UNITS * (n - 1))
                for h in range(HG):
                    for place_no, half_no in enumerate(order):
                        sp.dma_start(stacks[u][place_no * HD:(place_no + 1) * HD, h, :],
                                     qk_hl[what][h * HD:(h + 1) * HD, half_no, :]).then_inc(done[u], 16)

            def store_out(w, u):
                sp.wait_ge(sum_done, w + 1)
                sp.dma_start(out_t[bass.ds(w, 1)].rearrange("w p d -> p (w d)"), sum_sb[u][:]).then_inc(out_stored[u], 16)

            def attention_step(b, g, first=False, last=False, sums=True):
                n = G * b + g
                if not last:
                    for what in range(2):
                        stack(what, n + 1, g + 1, first)
                if sums and g == 0:
                    finish_batch(b - 1)

            def finish_batch(b, first=False):
                for j in range(J):
                    u = j % 2
                    if j >= 2:
                        store_out(J * b + j - 2, u)
                        sp.wait_ge(out_stored[u], 16 * (b * (J // 2) + j // 2))
                    elif not first:
                        sp.wait_ge(out_stored[u], 16 * (b * (J // 2)))
                    sp.dma_start(sum_sb[u][:], x_t[bass.ds(J * b + j, 1)].rearrange("w p d -> p (w d)")).then_inc(x_again[u], 16)
                for j in range(J - 2, J):
                    store_out(J * b + j, j % 2)

            for what in range(2):
                stack(what, 0, 0, True)
            for g in range(G):
                attention_step(0, g, first=g == 0, sums=False)
            for g in range(G):
                n = G + g
                for what in range(2):
                    stack(what, n + 1, g + 1, False)
                if g == 0:
                    finish_batch(0, True)
            with sp.Fori(2, B - 1) as b:
                for g in range(G):
                    attention_step(b, g)
            for g in range(G):
                attention_step(B - 1, g, last=g == G - 1)
            finish_batch(B - 1)
            for u in range(2):
                sp.wait_ge(out_stored[u], 16 * (NT // 2))

        @block.gpsimd
        def _(pool):
            own = Steps(pool, pool_own)
            own.link(pool.memset(zero_i[:], 0))
            own.link(pool.memset(ident16[:], 0.0))
            own.link(pool.memset(ident32[:], 0.0))
            own.link(pool.memset(ones16[:], 1.0))
            own.link(pool.memset(causal[:], 0.0))
            own.link(pool.affine_select(out=ident16[:], in_=ident16[:], compare_op=ALU.not_equal, fill=1.0,
                                        base=0, pattern=[[-1, P]], channel_multiplier=1))
            own.link(pool.affine_select(out=ident32[:], in_=ident32[:], compare_op=ALU.not_equal, fill=1.0,
                                        base=0, pattern=[[-1, P]], channel_multiplier=1))
            own.link(pool.affine_select(out=before16[:], in_=ones16[:], compare_op=ALU.is_gt, fill=0.0,
                                        base=0, pattern=[[1, P]], channel_multiplier=-1))
            own.link(pool.affine_select(out=causal[:], in_=causal[:], compare_op=ALU.is_ge, fill=MASKED,
                                        base=0, pattern=[[-1, P]], channel_multiplier=1))
            for u in range(2):
                last = pool.iota(token_no[u][:], [[P, J]], base=u * S, channel_multiplier=1)
                own.link(last) if u == 0 else last.then_inc(consts_made, 1)

            pool.wait_ge(amax_done, 1)
            pool.partition_all_reduce(amax_all[:, GM:GM + 1], amax[:, GM:GM + 1], P, bass.bass_isa.ReduceOp.max)\
                .then_inc(amax_everywhere, 1)

            def split(b, u):
                wait_apart(pool, amax_done, b + 2)
                pool.partition_all_reduce(amax_all[:, u:u + 1], amax[:, u:u + 1], P, bass.bass_isa.ReduceOp.max)\
                    .then_inc(amax_everywhere, 1)
                pool.wait_ge(x_hi_done, b + 1)
                pool.tensor_tensor(x_hl[u][:, :, 1, :], x_n[:], x_hl[u][:, :, 0, :], ALU.subtract).then_inc(x_lo_done, 1)

            def scatter(b, u, half_b):
                wait_apart(pool, target_done, b + 1)
                for j in range(J):
                    for k in range(2):
                        pool.indirect_dma_start(slot_table, bass.IndirectOffsetOnAxis(ap=target[u][:, k, j:j + 1], axis=0),
                                                token_no[u][:, j:j + 1], None).then_inc(scattered[u], 16)
                wait_apart(pool, scattered[u], 16 * 2 * J * (half_b + 1))
                own.link(pool.tensor_scalar(token_no[u][:], token_no[u][:], float(2 * S), None, ALU.add))

            split(0, 0)
            pool.wait_ge(table_zero, 16)
            own.enter(2)
            with pool.Fori(0, B // 2 - 1) as i:
                own.turn(i)
                split(2 * i + 1, 1)
                scatter(2 * i, 0, i)
                split(2 * i + 2, 0)
                scatter(2 * i + 1, 1, i)
            own.leave(B // 2 - 1)
            split(B - 1, 1)
            scatter(B - 2, 0, B // 2 - 1)
            scatter(B - 1, 1, B // 2 - 1)

            for m in range(E, NM):
                pool.wait_ge(amax_done, m + 2)
                pool.partition_all_reduce(amax_all[:, m:m + 1], amax[:, m:m + 1], P, bass.bass_isa.ReduceOp.max)\
                    .then_inc(amax_everywhere, 1)

            pool.wait_ge(table_loaded, 16)
            pool.wait_ge(tiles_done, 1)
            pool.wait_ge(w_lo_done, NM + 1)

            def gather(s, u, turn, first=False):
                col = pool.value_load(exp_col[0:1, 1, bass.ds(s, 1)], min_val=0, max_val=NCOL - 1)
                if not first:
                    pool.wait_ge(gathered[u], 16 * turn)
                    pool.wait_ge(xg_turned, s - 3)
                own.link(pool.tensor_copy(idx[u][:], tok_of[:, bass.ds(col, 1)]), wait_apart)
                pool.indirect_dma_start(x_g[u][:], None, xn_rows, bass.IndirectOffsetOnAxis(ap=idx[u][:], axis=0))\
                    .then_inc(gathered[u], 16)

            for u in range(4):
                gather(u, u, 0, True)
            own.enter(4)
            with pool.Fori(1, NTILE // 4) as i:
                own.turn(i - 1)
                for u in range(4):
                    gather(4 * i + u, u, i)
            own.leave(NTILE // 4 - 1)

            def rope(what, n):
                w = 2 * n + what
                pool.wait_ge(qk_rotated, w + 1)
                own.link(pool.tensor_tensor(turned[what][:], turned[what][:], trig_sb[:, 1, :], ALU.mult))
                pool.tensor_tensor(plain[what][:], plain[what][:], turned[what][:], ALU.add).then_inc(qk_roped, 1)

            def low_qk(what, n):
                pool.wait_ge(qk_hi, 2 * n + what + 1)
                pool.tensor_tensor(qk_hl[what][:, 1, :], plain[what][:], qk_hl[what][:, 0, :], ALU.subtract).then_inc(qk_lo, 1)

            def low_o(n, g):
                pool.wait_ge(o_hi, n + 1)
                pool.tensor_tensor(o_hl[:, g, 1, :], o_sb[:], o_hl[:, g, 0, :], ALU.subtract).then_inc(o_lo, 1)

            def gather_y(b, j, first=False):
                u, w = j % 2, J * b + j
                if not (first and j < 2):
                    pool.wait_ge(sum_done, w - 1)
                own.link(pool.tensor_copy(idx_y[u][:], slots[:, :, bass.ds(w, 1)].rearrange("p k w -> p (k w)")), wait_apart)
                for k in range(2):
                    pool.indirect_dma_start(y_in[u][:, k, :], None, y_rows, bass.IndirectOffsetOnAxis(ap=idx_y[u][:, k:k + 1], axis=0))\
                        .then_inc(y_back[u], 16)

            def attention_step(b, g, prev=True, nxt=True, sums=True, first_sums=False):
                n = G * b + g
                if nxt:
                    rope(0, n + 1)
                if prev:
                    low_o(n - 1, (g - 1) % G)
                if nxt:
                    low_qk(0, n + 1)
                    rope(1, n + 1)
                    low_qk(1, n + 1)
                if sums and g == 0:
                    for j in range(J):
                        gather_y(b - 1, j, first_sums)

            pool.wait_ge(trig_in, 16)
            pool.wait_ge(slots_final, 1)
            for u in range(4):
                pool.wait_ge(y_stored[u], 16 * (NTILE // 4))
            for what in range(2):
                rope(what, 0)
                low_qk(what, 0)
            for g in range(G):
                attention_step(0, g, prev=g > 0, sums=False)
            for g in range(G):
                attention_step(1, g, first_sums=True)
            own.enter(2 * G + J)
            with pool.Fori(2, B - 1) as b:
                own.turn(b - 2)
                for g in range(G):
                    attention_step(b, g)
            own.leave(B - 3)
            for g in range(G):
                attention_step(B - 1, g, nxt=g < G - 1)
            low_o(N - 1, G - 1)
            for j in range(J):
                gather_y(B - 1, j)

        @block.scalar
        def _(act):
            act.wait_ge(scale_done, 1)
            act.activation(gate_hl[:, :, 0:E], gate_f[:], ACT.Identity, scale=up[:, GM:GM + 1].bitcast(F32)).then_inc(w_hi_done, 1)

            def batch(b, u, half_b, first=False):
                act.wait_ge(var_done, b + 1)
                act.activation(std[:], var_eps[:], ACT.Sqrt).then_inc(std_done, 1)
                act.wait_ge(xn_done, b + 1)
                if not first:
                    act.wait_ge(xn_stored[u], 16 * half_b)
                    act.wait_ge(xt_done, J * (b - 1))
                act.activation(x_hl[u][:, :, 0, :], x_n[:], ACT.Copy).then_inc(x_hi_done, 1)
                act.wait_ge(scale_done, b + 2)
                act.activation(w_exp[:, bass.ds(b, 1), 0, :, :].rearrange("p m c d -> p (m c) d"), w_in[u][:], ACT.Identity,
                               scale=up[:, bass.ds(b, 1)].bitcast(F32)).then_inc(w_hi_done, 1)
                for j in range(J):
                    act.wait_ge(xt_done, J * b + j + 1)
                    act.activation(xT[:, :, bass.ds(b * S + j * P, P)],
                                   half(BANK_XT + j).rearrange("p (c t) -> p c t", t=P), ACT.Copy).then_inc(xT_copied, 1)

            batch(0, 0, 0, True)
            batch(1, 1, 0, True)
            with act.Fori(1, B // 2) as i:
                for u in range(2):
                    batch(2 * i + u, u, i)

            act.wait_ge(gap_done, B)
            act.activation(w12[:, 1, :], gap[:], ACT.Exp, scale=down[:, GM:GM + 1].bitcast(F32)).then_inc(gap_exp, 1)
            act.wait_ge(bias_loaded, 16)
            for m in range(E, NM):
                act.wait_ge(scale_done, m + 2)
                act.activation(w_att[:, m - E, 0, :, :], wq_in[m % 2][:], ACT.Identity,
                               scale=up[:, m:m + 1].bitcast(F32)).then_inc(w_hi_done, 1)

            def copy_xgT(s, u, first=False):
                act.wait_ge(xg_turned, s + 1)
                if not first:
                    act.wait_ge(y_done, s - 1)
                act.activation(x_gT[u][:], half(u).rearrange("p (c t) -> p c t", t=P), ACT.Copy).then_inc(xgT_copied, 1)

            act.wait_ge(w_lo_done, NM + 1)
            for u in range(2):
                copy_xgT(u, u, True)
            with act.Fori(1, NTILE // 2) as i:
                for u in range(2):
                    copy_xgT(2 * i + u, u)

            def high_qk(what, n):
                act.wait_ge(qk_roped, 2 * n + what + 1)
                act.activation(qk_hl[what][:, 0, :], plain[what][:], ACT.Copy).then_inc(qk_hi, 1)

            def stacked(what, b, g):
                done = (q_stacked, k_stacked)[what][g % 2]
                act.wait_ge(done, 16 * 4 * HG * (b * (G // 2) + g // 2 + 1))

            def take_v(n, g, prev):
                act.wait_ge(v_summed, n + 1)
                if prev:
                    act.wait_ge(pv_done, n - 1)
                act.activation(v_sb[g % 2][:], banks[BANK_O][:].rearrange("p (j d) -> p j d", j=J), ACT.Copy,
                               scale=2.0 ** -LOG_V).then_inc(v_read, 1)

            def exps(b, g, k, free=True):
                n, i, pair = G * b + g, k // 2, k % 2
                W = (i + 1) * P
                act.wait_ge(shift_done, UNITS * n + k + 1)
                if free:
                    act.wait_ge(pt_turned, (fill(n, fills(k - 2)[-1]) if k >= 2 else fill(n, fills(7)[-1]) if k == 1
                                            else fill(n - 1, fills(6)[-1])) + 1)
                for h in range(2):
                    last = act.activation(p_sb[k % 2][:, h, 0:W], banks[BANK_S + 2 * (k % 2) + h][:, 0:W], ACT.Exp,
                                          bias=shift[:, k % 2, h:h + 1], scale=factors[:, 0:1],
                                          accum_out=den[g % 2][:, i, 2 * pair + h:2 * pair + h + 1])
                last.then_inc(exp_done, 1)

            def copy_pt(b, g, k, a):
                n = G * b + g
                bank = pt_bank(g, a)
                act.wait_ge(pt_turned, fill(n, a) + 1)
                _, view, to = part(k, a)
                act.activation(to, view(banks[BANK_PT + bank]), ACT.Copy).then_inc(pt_copied[bank], 1)

            def attention_step(b, g, prev=True, nxt=True):
                n = G * b + g
                exps(b, g, 0, prev)
                if prev:
                    copy_pt(b, g, 7, 1)
                exps(b, g, 1, prev)
                if prev:
                    bank = pt_bank(g, FILL_R)
                    act.wait_ge(pt_turned, fill(n, FILL_R) + 1)
                    if not (isinstance(n, int) and n == 1):
                        act.wait_ge(o_lo, n - 1)
                    act.activation(o_sb[:], banks[BANK_PT + bank][:], ACT.Copy).then_inc(pt_copied[bank], 1)
                exps(b, g, 2)
                if prev:
                    act.wait_ge(o_read, n)
                    if g == 1:
                        act.wait_ge(wo_done, J * b)
                    act.activation(o_hl[:, (g - 1) % G, 0, :], o_sb[:], ACT.Copy).then_inc(o_hi, 1)
                exps(b, g, 3)
                if nxt:
                    stacked(0, b, g)
                    high_qk(0, n + 1)
                exps(b, g, 4)
                if prev:
                    act.wait_ge(pv_done, n)
                copy_pt(b, g, 3, 6)
                exps(b, g, 5)
                if nxt:
                    stacked(1, b, g)
                    high_qk(1, n + 1)
                copy_pt(b, g, 4, 8)
                exps(b, g, 6)
                copy_pt(b, g, 5, 10)
                exps(b, g, 7)
                copy_pt(b, g, 6, 12)
                if nxt:
                    take_v(n + 1, g + 1, prev)

            act.wait_ge(y_scaled, NTILE)
            for what in range(2):
                high_qk(what, 0)
            take_v(0, 0, False)
            act.wait_ge(factors_done, 1)
            for g in range(G):
                attention_step(0, g, prev=g > 0)
            with act.Fori(1, B - 1) as b:
                for g in range(G):
                    attention_step(b, g)
            for g in range(G):
                attention_step(B - 1, g, nxt=g < G - 1)
            copy_pt(B, 0, 7, 1)
            bank = pt_bank(0, FILL_R)
            act.wait_ge(pt_turned, fill(N, FILL_R) + 1)
            act.wait_ge(o_lo, N - 1)
            act.activation(o_sb[:], banks[BANK_PT + bank][:], ACT.Copy).then_inc(pt_copied[bank], 1)
            act.wait_ge(o_read, N)
            act.activation(o_hl[:, G - 1, 0, :], o_sb[:], ACT.Copy).then_inc(o_hi, 1)

        @block.tensor
        def _(pe):
            pe.wait_ge(consts_made, 1)

            def ranks(b, v, first=False):
                bank = banks[BANK_RANK + v]
                pe.wait_ge(chosen_done, b + 1)
                if not first:
                    pe.wait_ge(rank_read, b - 1)
                for j in range(J + 1):
                    o = bank[:, j * E:(j + 1) * E]
                    for k in range(j + (j < J)):
                        now = pe.matmul(o, before16[:] if k == j else ones16[:], chosen[:, k * E:(k + 1) * E],
                                        start=k == 0, stop=k == min(j, J - 1))
                now.then_inc(rank_done, 1)

            def turn_x(b, u, first=False):
                pe.wait_ge(x_lo_done, b + 1)
                for j in range(J):
                    if not first:
                        pe.wait_ge(xT_copied, J * (b - 1) + j + 1)
                    for c in range(2 * C):
                        now = pe.transpose(half(BANK_XT + j)[:, c * P:(c + 1) * P],
                                           x_hl[u][:, j, c // C, c % C * P:(c % C + 1) * P], ident16[:])
                    now.then_inc(xt_done, 1)

            def gate_logits(b, v, first=False):
                bank = banks[BANK_GATE + v]
                pe.wait_ge(xT_copied, J * (b + 1))
                if not first:
                    pe.wait_ge(logit_read, b - 1)
                for j in range(J):
                    toks = bass.ds(b * S + j * P, P)
                    o = bank[:, j * 2 * E:(j + 1) * 2 * E]
                    pe.matmul(o, xT[:, 0, toks], gate_hl[:, 0, :], start=True, stop=False)
                    for c in range(C):
                        pe.matmul(o[:, 0:E], xT[:, C + c, toks], gate_hl[:, c, 0:E], start=False, stop=False)
                    for c in range(1, C):
                        now = pe.matmul(o, xT[:, c, toks], gate_hl[:, c, :], start=False, stop=c == C - 1)
                now.then_inc(gate_done, 1)

            turn_x(0, 0, True)
            pe.wait_ge(w_lo_done, 1)
            gate_logits(0, 0, True)
            ranks(0, 0, True)
            turn_x(1, 1)
            gate_logits(1, 1, True)
            ranks(1, 1, True)
            turn_x(2, 0)
            gate_logits(2, 0)
            with pe.Fori(1, B // 2 - 1) as i:
                for v in range(2):
                    ranks(2 * i + v, v)
                    turn_x(2 * i + v + 1, 1 - v)
                    gate_logits(2 * i + v + 1, 1 - v)
            ranks(B - 2, 0)
            turn_x(B - 1, 1)
            gate_logits(B - 1, 1)
            ranks(B - 1, 1)

            def turn_xg(s, u4, u2, turn, first=False):
                pe.wait_ge(gathered[u4], 16 * (turn + 1))
                if not first:
                    pe.wait_ge(xgT_copied, s - 1)
                for c in range(2 * C):
                    now = pe.transpose(half(u2)[:, c * P:(c + 1) * P], x_g[u4][:, c * P:(c + 1) * P], ident16[:])
                now.then_inc(xg_turned, 1)

            def expert(s, u, first=False):
                e = pe.value_load(exp_col[0:1, 0, bass.ds(s, 1)], min_val=0, max_val=E - 1)
                pe.wait_ge(xgT_copied, s + 1)
                if not first:
                    pe.wait_ge(y_scaled, s - 1)
                n = 0
                for c in range(C):
                    for xp, wp in ((0, 0), (0, 1), (1, 0)):
                        now = pe.matmul(banks[4 + u][:], x_gT[u][:, xp * C + c, :],
                                        w_exp[:, bass.ds(e, 1), wp, c, :].rearrange("p e d -> p (e d)"),
                                        start=n == 0, stop=n == 3 * C - 1)
                        n += 1
                now.then_inc(y_done, 1)

            pe.wait_ge(tiles_done, 1)
            pe.wait_ge(w_lo_done, NM + 1)
            turn_xg(0, 0, 0, 0, True)
            for s in range(4):
                turn_xg(s + 1, (s + 1) % 4, (s + 1) % 2, (s + 1) // 4, s == 0)
                expert(s, s % 2, s < 2)
            with pe.Fori(1, NTILE // 4 - 1) as i:
                for u in range(4):
                    turn_xg(4 * i + u + 1, (u + 1) % 4, (u + 1) % 2, i + (u + 1) // 4)
                    expert(4 * i + u, u % 2)
            for s in range(NTILE - 4, NTILE):
                if s + 1 < NTILE:
                    turn_xg(s + 1, (s + 1) % 4, (s + 1) % 2, (s + 1) // 4)
                expert(s, s % 2)

            def scores(b, g, k, free=True):
                n, i, pair = G * b + g, k // 2, k % 2
                W = (i + 1) * P
                if free:
                    pe.wait_ge(exp_done, UNITS * n + k - 1)
                for h in range(2):
                    o, head = banks[BANK_S + 2 * (k % 2) + h], 2 * pair + h
                    pe.matmul(o[:, 0:W], q_stack[g % 2][:, head, i * P:(i + 1) * P], k_stack[g % 2][:, head, 0:W],
                              start=True, stop=False)
                    last = pe.matmul(o[:, W - P:W], ident16[:], causal[:], start=False, stop=True)
                last.then_inc(scores_done, 1)

            def turn_p(b, g, k):
                n = G * b + g
                pe.wait_ge(exp_done, UNITS * (n - 1 if k == 7 else n) + k + 1)
                for a in fills(k):
                    bank = pt_bank(g, a)
                    wait = fills_up_to(bank, b, g, a) - 1
                    if not isinstance(wait, int) or wait > 0:
                        pe.wait_ge(pt_copied[bank], wait)
                    blocks, _, _ = part(k, a)
                    for head, j, col in blocks:
                        last = pe.transpose(banks[BANK_PT + bank][:, col:col + P], p_sb[k % 2][:, head % 2, j * P:(j + 1) * P], ident32[:])
                    last.then_inc(pt_turned, 1)

            def times_v(b, g, wo_tiles, nxt=True):
                n = G * b + g
                for bank in range(2):
                    pe.wait_ge(pt_copied[bank], fills_up_to(bank, b, g, 1))
                pe.wait_ge(v_read, n + 1 if nxt else n)
                if wo_tiles is not None:
                    pe.wait_ge(wo_read, wo_tiles)
                for j in range(J):
                    for h in range(HG):
                        last = pe.matmul(banks[BANK_O][h * HD:(h + 1) * HD, j * P:S], v_sb[(g - 1) % 2][:, j, h * HD:(h + 1) * HD],
                                         pT[:, h, j, j * P:S], start=j == 0, stop=j == J - 1)
                last.then_inc(pv_done, 1)
                bank = pt_bank(g, FILL_R)
                pe.wait_ge(rden_done, n)
                pe.wait_ge(pt_copied[bank], fills_up_to(bank, b, g, FILL_R) - 1)
                for i in range(J):
                    last = pe.transpose(banks[BANK_PT + bank][:, i * P:(i + 1) * P],
                                        rden[:, i].rearrange("p h d -> p (h d)"), ident32[:])
                last.then_inc(pt_turned, 1)

            PASSES = ((0, 0), (0, 1), (1, 0))

            def project_qk(what, b, g, free):
                pieces = []
                for c in range(C):
                    for m, (xp, wp) in enumerate(PASSES):
                        def piece(c=c, m=m, xp=xp, wp=wp):
                            if c == 0 and m == 0 and free:
                                for s_, v_ in free:
                                    pe.wait_ge(s_, v_)
                            now = pe.matmul(banks[BANK_Q][:], w_att[:, what, wp, c, g * P:(g + 1) * P],
                                            xT[:, xp * C + c, bass.ds(b * S, S)],
                                            start=c == 0 and m == 0, stop=c == C - 1 and m == 2)
                            if c == C - 1 and m == 2:
                                now.then_inc(qk_summed, 1)
                        pieces.append(piece)
                return pieces

            def project_v(b, g, free):
                pieces = []
                for j in range(J):
                    for m, (xp, wp) in enumerate(PASSES):
                        def piece(j=j, m=m, xp=xp, wp=wp):
                            if j == 0 and m == 0 and free:
                                for s_, v_ in free:
                                    pe.wait_ge(s_, v_)
                            for c in range(C):
                                now = pe.matmul(banks[BANK_O][:, j * P:(j + 1) * P], xT[:, xp * C + c, bass.ds(b * S + j * P, P)],
                                                w_att[:, 2, wp, c, g * P:(g + 1) * P],
                                                start=m == 0 and c == 0, stop=m == 2 and c == C - 1)
                            if j == J - 1 and m == 2:
                                now.then_inc(v_summed, 1)
                        pieces.append(piece)
                return pieces

            def project_out(b, j, free):
                pieces = []
                for c in range(C):
                    for m, (xp, wp) in enumerate(PASSES):
                        def piece(c=c, m=m, xp=xp, wp=wp):
                            if c == 0 and m == 0:
                                pe.wait_ge(o_lo, G * (b + 1))
                                for s_, v_ in free:
                                    pe.wait_ge(s_, v_)
                            now = pe.matmul(banks[BANK_MISC + j % 2][:], o_hl[:, c, xp, j * P:(j + 1) * P], w_att[:, 3, wp, c, :],
                                            start=c == 0 and m == 0, stop=c == C - 1 and m == 2)
                            if c == C - 1 and m == 2:
                                now.then_inc(wo_done, 1)
                        pieces.append(piece)
                return pieces

            def out_tiles(b, n):
                pieces = []
                for j in range(J):
                    free = [[(qk_rotated, 2 * n + 2)], [(v_read, n + 1)]][j] if j < 2 else [(wo_read, J * b + j - 1)]
                    pieces += project_out(b, j, free)
                return pieces

            def attention_step(b, g, prev=True, nxt=True, sums=True):
                n = G * b + g
                bq, gq = (b, g + 1) if g + 1 < G else (b + 1, 0)
                fillers = [[] for _ in range(UNITS)]
                if nxt:
                    q_free = [(qk_rotated, 2 * n + 2)]
                    if sums and g == 1:
                        q_free.append((wo_read, J * (b - 1) + J - 1))
                    qs = project_qk(0, bq, gq, q_free)
                    ks = project_qk(1, bq, gq, [(qk_rotated, 2 * n + 3)])
                    vs = project_v(bq, gq, [(o_read, n)] if prev else [(v_read, 1)])
                    qk = qs + ks
                    fillers[0], fillers[2], fillers[3] = qk[:8], qk[8:12], qk[12:20]
                    fillers[4], fillers[5], fillers[6], fillers[7] = qk[20:] + vs[:2], vs[2:5], vs[5:9], vs[9:]
                if sums and g == 0:
                    outs = out_tiles(b - 1, n + 1)
                    tail = outs
                else:
                    tail = []
                for k in range(UNITS):
                    if k == 0:
                        for done in (q_stacked, k_stacked):
                            pe.wait_ge(done[g % 2], 16 * 4 * HG * (b * (G // 2) + g // 2 + 1))
                    scores(b, g, k, not (isinstance(n, int) and n == 0 and k < 2))
                    if k == 1 and prev:
                        times_v(b, g, J * (b - 1) + J if sums and g == 1 else None)
                    for piece in fillers[k]:
                        piece()
                    if k == 0:
                        if prev:
                            turn_p(b, g, 7)
                    else:
                        turn_p(b, g, k - 1)
                for piece in tail:
                    piece()

            pe.wait_ge(xgT_copied, NTILE)
            pe.wait_ge(w_lo_done, NM + 1)
            for piece in project_qk(0, 0, 0, []) + project_qk(1, 0, 0, [(qk_rotated, 1)]) + project_v(0, 0, []):
                piece()
            pe.wait_ge(y_scaled, NTILE)
            for g in range(G):
                attention_step(0, g, prev=g > 0, sums=False)
            with pe.Fori(1, B - 1) as b:
                for g in range(G):
                    attention_step(b, g)
            for g in range(G):
                attention_step(B - 1, g, nxt=g < G - 1)
            turn_p(B, 0, 7)
            times_v(B, 0, None, nxt=False)
            for j in range(J):
                for piece in project_out(B - 1, j, [(o_read, N)] if j < 2 else [(wo_read, J * (B - 1) + j - 1)]):
                    piece()

        @block.vector
        def _(dve):
            own = Steps(dve, dve_own)
            own.link(dve.memset(gap[:], 0.0))
            dve.wait_ge(const_in, 16)
            own.link(dve.tensor_copy(carry[:], first_row))
            dve.wait_ge(gate_in, 16)
            dve.tensor_reduce(out=amax[:, GM:GM + 1], in_=gate_f[:], axis=AX.XY, op=ALU.max, apply_absolute_value=True).then_inc(amax_done, 1)
            dve.wait_ge(amax_everywhere, 1)
            scale_ops(dve, own, bass.ds(GM, 1)).then_inc(scale_done, 1)
            dve.wait_ge(w_hi_done, 1)
            dve.scalar_tensor_tensor(gate_hl[:, :, E:2 * E], gate_f[:], up[:, GM:GM + 1].bitcast(F32), gate_hl[:, :, 0:E],
                                     ALU.mult, ALU.subtract).then_inc(w_lo_done, 1)

            def normalise(b, u, half_b, first=False):
                dve.wait_ge(x_loaded[u], 16 * (half_b + 1))
                for j in range(J):
                    now = dve.bn_stats(stats[:, j, :], x_in[u][:, j, :])
                own.link(now, wait_apart)
                for j in range(J):
                    now = dve.bn_aggr(mean_var[:, j, :], stats[:, j, :])
                own.link(now)
                dve.tensor_scalar(var_eps[:], mean_var[:, :, 1], EPS, None, ALU.add).then_inc(var_done, 1)
                dve.wait_ge(w_loaded[u], 16 * (half_b + 1))
                dve.tensor_reduce(out=amax[:, u:u + 1], in_=w_in[u][:], axis=AX.XY, op=ALU.max, apply_absolute_value=True).then_inc(amax_done, 1)
                dve.wait_ge(std_done, b + 1)
                own.link(dve.reciprocal(r0[:], std[:]))
                own.link(dve.tensor_tensor(r1[:], r0[:], r0[:], ALU.mult))
                own.link(dve.tensor_tensor(r1[:], r1[:], var_eps[:], ALU.mult))
                own.link(dve.tensor_scalar(r1[:], r1[:], -0.5, 1.5, ALU.mult, ALU.add))
                own.link(dve.scalar_tensor_tensor(rstd[:], r0[:], float(2 ** LOG_X), r1[:], ALU.mult, ALU.mult))
                if not first:
                    dve.wait_ge(x_hi_done, b)
                    dve.wait_ge(x_lo_done, b)
                for j in range(J):
                    now = dve.tensor_scalar(x_n[:, j, :], x_in[u][:, j, :], mean_var[:, j, 0:1], rstd[:, j:j + 1],
                                            ALU.subtract, ALU.mult)
                now.then_inc(xn_done, 1)
                dve.wait_ge(amax_everywhere, b + 2)
                scale_ops(dve, own, bass.ds(b, 1), slice(u, u + 1)).then_inc(scale_done, 1)

            def low_part(b, u):
                dve.wait_ge(w_hi_done, b + 2)
                dve.scalar_tensor_tensor(w_exp[:, bass.ds(b, 1), 1, :, :].rearrange("p m c d -> p (m c d)"),
                                         w_in[u][:].rearrange("p c d -> p (c d)"), up[:, bass.ds(b, 1)].bitcast(F32),
                                         w_exp[:, bass.ds(b, 1), 0, :, :].rearrange("p m c d -> p (m c d)"),
                                         ALU.mult, ALU.subtract).then_inc(w_lo_done, 1)

            def over_e(ap):
                return ap.unsqueeze(2).broadcast_to([P, J, E])

            def route(b, u, half_b, first=False):
                dve.wait_ge(gate_done, b + 1)
                dve.tensor_reduce(out=logit[:], in_=banks[BANK_GATE + u][:, 0:2 * E * J].rearrange("p (j h e) -> p j e h", h=2, e=E),
                                  axis=AX.X, op=ALU.add).then_inc(logit_read, 1)
                dve.wait_ge(logit_read, b + 1)
                for k, of in enumerate((logit, rest)):
                    own.link(dve.tensor_reduce(out=best[:, k, :], in_=of[:], axis=AX.X, op=ALU.max))
                    own.link(dve.tensor_tensor(same[:], of[:], over_e(best[:, k, :]), ALU.is_equal))
                    own.link(dve.tensor_tensor(same[:], same[:], prefer, ALU.mult))
                    own.link(dve.tensor_reduce(out=rank[:], in_=same[:], axis=AX.X, op=ALU.max))
                    own.link(dve.tensor_tensor(one_hot[k][:], same[:], over_e(rank[:]), ALU.is_equal))
                    if k == 0:
                        own.link(dve.scalar_tensor_tensor(rest[:], one_hot[0][:], MASKED, logit[:], ALU.mult, ALU.add))
                if not first:
                    dve.wait_ge(rank_done, b)
                dve.tensor_tensor(chosen[:].rearrange("p (j e) -> p j e", j=J), one_hot[0][:], one_hot[1][:], ALU.add)\
                    .then_inc(chosen_done, 1)
                dve.tensor_tensor(gap[:, bass.ds(b * J, J)], best[:, 1, :], best[:, 0, :], ALU.subtract).then_inc(gap_done, 1)
                dve.wait_ge(rank_done, b + 1)
                own.link(dve.tensor_tensor(place_f[:], banks[BANK_RANK + u][:, 0:J * E].rearrange("p (j e) -> p j e", j=J),
                                           carry[:].unsqueeze(1).broadcast_to([P, J, E]), ALU.add))
                dve.tensor_tensor(carry[:], banks[BANK_RANK + u][:, J * E:(J + 1) * E], carry[:], ALU.add).then_inc(rank_read, 1)
                dve.wait_ge(rank_read, b + 1)
                for k in range(2):
                    own.link(dve.tensor_tensor(picked[:, k], one_hot[k][:], place_f[:], ALU.mult))
                own.link(dve.tensor_reduce(out=slot_f[:], in_=picked[:], axis=AX.X, op=ALU.add))
                here = slots[:, :, bass.ds(b * J, J)]
                own.link(dve.tensor_copy(here, slot_f[:]))
                own.link(dve.tensor_scalar(low7[:], here, P - 1, None, ALU.bitwise_and))
                own.link(dve.tensor_scalar(high[:], here, 7, None, ALU.logical_shift_right))
                if not first:
                    dve.wait_ge(scattered[u], 16 * 2 * J * half_b)
                dve.scalar_tensor_tensor(target[u][:], low7[:], float(NCOL), high[:], ALU.mult, ALU.add).then_inc(target_done, 1)

            LINKS = 2 + 5 + 3 + 11 + 1 + 2 + 1 + 3
            normalise(0, 0, 0, True)
            low_part(0, 0)
            normalise(1, 1, 0)
            route(0, 0, 0, True)
            low_part(1, 1)
            normalise(2, 0, 1)
            route(1, 1, 0, True)
            low_part(2, 0)
            own.enter(2 * LINKS)
            with dve.Fori(1, B // 2 - 1) as i:
                own.turn(i - 1)
                normalise(2 * i + 1, 1, i)
                route(2 * i, 0, i)
                low_part(2 * i + 1, 1)
                normalise(2 * i + 2, 0, i + 1)
                route(2 * i + 1, 1, i)
                low_part(2 * i + 2, 0)
            own.leave(B // 2 - 2)
            normalise(B - 1, 1, B // 2 - 1)
            route(B - 2, 0, B // 2 - 1)
            low_part(B - 1, 1)
            route(B - 1, 1, B // 2 - 1)

            for u in range(2):
                dve.wait_ge(xn_stored[u], 16 * (B // 2))
                dve.wait_ge(scattered[u], 16 * J * B)
            dve.wait_ge(xt_done, NT)
            own.link(dve.tensor_tensor(tiles[:], carry[:], first_row, ALU.subtract))
            own.link(dve.tensor_scalar(cnt_i[:], tiles[:], float(P - 1), None, ALU.add))
            own.link(dve.tensor_scalar(cnt_i[:], cnt_i[:], 7, None, ALU.logical_shift_right))
            own.link(dve.tensor_copy(tiles[:], cnt_i[:]))
            own.link(dve.tensor_copy(ends[:, 0, :], tiles[:]))
            for n in (1, 2, 4):
                a, z = (0, 1) if n != 2 else (1, 0)
                own.link(dve.tensor_copy(ends[:, z, 0:n], ends[:, a, 0:n]))
                own.link(dve.tensor_tensor(ends[:, z, n:E], ends[:, a, n:E], ends[:, a, 0:E - n], ALU.add))
            both = [P, NTILE, E]
            own.link(dve.tensor_tensor(past[:], tile_no.unsqueeze(2).broadcast_to(both), ends[:, 1, :].unsqueeze(1).broadcast_to(both),
                                       ALU.is_ge))
            own.link(dve.tensor_reduce(out=n_past[:], in_=past[:], axis=AX.X, op=ALU.add))
            own.link(dve.tensor_tensor(past[:], past[:], tiles[:].unsqueeze(1).broadcast_to(both), ALU.mult))
            own.link(dve.tensor_reduce(out=t_past[:], in_=past[:], axis=AX.X, op=ALU.add))
            own.link(dve.tensor_tensor(t_col[:], tile_no, t_past[:], ALU.subtract))
            own.link(dve.scalar_tensor_tensor(exp_col[:, 1, :], n_past[:], float(NT), t_col[:], ALU.mult, ALU.add))
            dve.tensor_scalar(exp_col[:, 0, :], n_past[:], float(E - 1), None, ALU.min).then_inc(tiles_done, 1)

            own.link(dve.tensor_tensor(moves[:], ends[:, 1, :], tiles[:], ALU.subtract))
            own.link(dve.scalar_tensor_tensor(moves[:], moves[:], float(P), first_row, ALU.mult, ALU.subtract))
            own.link(dve.tensor_scalar(slot_i[:], slots[:], (NT * P).bit_length() - 1, None, ALU.logical_shift_right))
            own.link(dve.tensor_copy(slot_e[:], slot_i[:]))
            own.link(dve.tensor_copy(slot_now[:], slots[:]))
            for e in range(E):
                own.link(dve.tensor_scalar(move[:], slot_e[:], float(e), moves[:, e:e + 1], ALU.is_equal, ALU.mult))
                own.link(dve.tensor_tensor(slot_now[:], slot_now[:], move[:], ALU.add))
            dve.tensor_copy(slots[:], slot_now[:]).then_inc(slots_final, 1)

            dve.wait_ge(gap_exp, 1)
            own.link(dve.tensor_scalar(w12[:, 0, :], w12[:, 1, :], 1.0, None, ALU.add))
            own.link(dve.reciprocal(w12[:, 0, :], w12[:, 0, :]))
            dve.tensor_tensor(w12[:, 1, :], w12[:, 1, :], w12[:, 0, :], ALU.mult).then_inc(w12_done, 1)

            def largest(m):
                dve.wait_ge(w_loaded[m % 2], 16 * (m // 2 + 1))
                dve.tensor_reduce(out=amax[:, m:m + 1], in_=wq_in[m % 2][:], axis=AX.XY, op=ALU.max, apply_absolute_value=True).then_inc(amax_done, 1)

            largest(E)
            for m in range(E, NM):
                dve.wait_ge(amax_everywhere, m + 2)
                scale_ops(dve, own, bass.ds(m, 1)).then_inc(scale_done, 1)
                if m + 1 < NM and m == E:
                    largest(m + 1)
                dve.wait_ge(w_hi_done, m + 2)
                dve.scalar_tensor_tensor(w_att[:, m - E, 1, :, :], wq_in[m % 2][:], up[:, m:m + 1].bitcast(F32),
                                         w_att[:, m - E, 0, :, :], ALU.mult, ALU.subtract).then_inc(w_lo_done, 1)
                if m + 2 < NM and m >= E:
                    largest(m + 2)

            dve.wait_ge(bias_loaded, 16)
            dve.wait_ge(w_lo_done, NM + 1)

            def scale_y(s, u, turn, first=False):
                e = dve.value_load(exp_col[0:1, 0, bass.ds(s, 1)], min_val=0, max_val=E - 1)
                dve.wait_ge(y_done, s + 1)
                if not first:
                    dve.wait_ge(y_stored[u], 16 * turn)
                dve.scalar_tensor_tensor(y_sb[u][:], banks[4 + u % 2][:], down[:, bass.ds(e, 1)].bitcast(F32),
                                         bias_all[:, bass.ds(e, 1), :].rearrange("p e d -> p (e d)"), ALU.mult, ALU.add)\
                    .then_inc(y_scaled, 1)

            for u in range(4):
                scale_y(u, u, 0, True)
            with dve.Fori(1, NTILE // 4) as i:
                for u in range(4):
                    scale_y(4 * i + u, u, i)

            q_, k_, v_, o_ = (down[:, m:m + 1].bitcast(F32) for m in range(E, NM))
            own.link(dve.tensor_tensor(factors[:, 0:1], q_, k_, ALU.mult))
            own.link(dve.tensor_scalar(factors[:, 0:1], factors[:, 0:1], 2.0 ** (2 * LOG_V) * HD ** -0.5, None, ALU.mult))
            own.link(dve.tensor_scalar(factors[:, 1:2], factors[:, 0:1], -1.0, None, ALU.mult))
            own.link(dve.tensor_tensor(factors[:, 2:3], v_, o_, ALU.mult))
            dve.tensor_scalar(factors[:, 2:3], factors[:, 2:3], 2.0 ** (LOG_V + LOG_X), None, ALU.mult).then_inc(factors_done, 1)
            for u in range(4):
                dve.wait_ge(y_stored[u], 16 * (NTILE // 4))
            dve.wait_ge(factors_done, 1)
            dve.wait_ge(trig_in, 16)

            swap = [(i + HD // 2) % HD for i in range(HD)]

            def rotate(what, n, first=False):
                w = 2 * n + what
                wait_apart(dve, qk_summed, w + 1)
                if not first:
                    wait_apart(dve, qk_lo, w - 1)
                dve.stream_shuffle(turned[what][:], banks[BANK_Q][:], swap)
                dve.tensor_tensor(plain[what][:], banks[BANK_Q][:], trig_sb[:, 0, :], ALU.mult).then_inc(qk_rotated, 1)

            def shifts(b, g, k):
                n, i = G * b + g, k // 2
                W = (i + 1) * P
                dve.wait_ge(scores_done, UNITS * n + k + 1)
                own.link(dve.tensor_reduce(out=top[:, k % 2, :], in_=s_banks(k % 2)[:, :, 0:W], axis=AX.X, op=ALU.max))
                dve.tensor_scalar(shift[:, k % 2, :], top[:, k % 2, :], factors[:, 1:2], None, ALU.mult).then_inc(shift_done, 1)

            def copy_pt(b, g, k, a):
                bank = pt_bank(g, a)
                dve.wait_ge(pt_turned, fill(G * b + g, a) + 1)
                _, view, to = part(k, a)
                dve.tensor_copy(to, view(banks[BANK_PT + bank])).then_inc(pt_copied[bank], 1)

            def reciprocals(n, g):
                dve.wait_ge(exp_done, UNITS * n)
                dve.reciprocal(rden[:].rearrange("p j h d -> p (j h) d"), den[(g - 1) % 2][:].rearrange("p j h -> p (j h)").unsqueeze(2).broadcast_to([P, J * HG, HD])).then_inc(rden_done, 1)

            def normalise_o(b, g):
                n, bank = G * b + g, pt_bank(g, FILL_R)
                dve.wait_ge(pv_done, n)
                dve.wait_ge(pt_copied[bank], fills_up_to(bank, b, g, FILL_R))
                dve.tensor_tensor(o_sb[:], banks[BANK_O][:], o_sb[:], ALU.mult).then_inc(o_read, 1)

            def add_up(b, j):
                u, w = j % 2, J * b + j
                dve.wait_ge(wo_done, w + 1)
                dve.wait_ge(x_again[u], 16 * (b * (J // 2) + j // 2 + 1))
                dve.scalar_tensor_tensor(sum_sb[u][:], banks[BANK_MISC + u], factors[:, 2:3], sum_sb[u][:], ALU.mult, ALU.add)\
                    .then_inc(wo_read, 1)
                dve.wait_ge(wo_read, w + 1)
                dve.wait_ge(y_back[u], 32 * (b * (J // 2) + j // 2 + 1))
                own.link(dve.scalar_tensor_tensor(sum_sb[u][:], y_in[u][:, 0, :], w12[:, 0, bass.ds(w, 1)], sum_sb[u][:], ALU.mult, ALU.add))
                dve.scalar_tensor_tensor(sum_sb[u][:], y_in[u][:, 1, :], w12[:, 1, bass.ds(w, 1)], sum_sb[u][:], ALU.mult, ALU.add)\
                    .then_inc(sum_done, 1)

            def attention_step(b, g, prev=True, nxt=True, sums=True):
                n = G * b + g
                if prev:
                    reciprocals(n, g)
                shifts(b, g, 0)
                if prev:
                    copy_pt(b, g, 7, 0)
                shifts(b, g, 1)
                if prev:
                    dve.wait_ge(pv_done, n)
                copy_pt(b, g, 0, 3)
                shifts(b, g, 2)
                if prev:
                    normalise_o(b, g)
                if nxt:
                    rotate(0, n + 1)
                copy_pt(b, g, 1, 4)
                shifts(b, g, 3)
                copy_pt(b, g, 2, 5)
                for k, a in ((4, None), (5, 7), (6, 9), (7, 11)):
                    shifts(b, g, k)
                    if k == 4 and nxt:
                        rotate(1, n + 1)
                    if a:
                        copy_pt(b, g, k - 1, a)
                if sums and g == 0:
                    for j in range(J):
                        add_up(b - 1, j)

            for what in range(2):
                rotate(what, 0, True)
            for g in range(G):
                attention_step(0, g, prev=g > 0, sums=False)
            own.enter(G * UNITS + J)
            with dve.Fori(1, B - 1) as b:
                own.turn(b - 1)
                for g in range(G):
                    attention_step(b, g)
            own.leave(B - 2)
            for g in range(G):
                attention_step(B - 1, g, nxt=g < G - 1)
            reciprocals(N, 0)
            copy_pt(B, 0, 7, 0)
            normalise_o(B, 0)
            for j in range(J):
                add_up(B - 1, j)


def kernel(**inputs):
    from concourse import bacc
    from concourse.bass_utils import run_bass_kernel_spmd

    a = {k: np.asarray(v) for k, v in inputs.items()}
    x = a["L0_attn_x"]
    B, S, D = x.shape
    E = a["L0_ffn_gate_w"].shape[0]
    J, C, T = S // P, D // P, B * S
    NTILE = -(-(2 * (T // P) + E - 1) // 4) * 4

    def chunks(w):
        return w.T.reshape(C, P, w.shape[0]).transpose(1, 0, 2)

    mats = [a["L0_ffn_expert_w"][e] for e in range(E)] + [a["L0_attn_" + n] for n in ("Wq", "Wk", "Wv", "Wo")]
    HEAD = D // 16
    inv_freq = (np.float32(1.0) / np.power(np.float32(10000.0), np.arange(0, HEAD, 2, dtype=np.float32) / np.float32(HEAD))).astype(np.float32)
    freqs = np.outer(np.arange(S, dtype=np.float32), inv_freq).astype(np.float32)
    emb = np.concatenate([freqs, freqs], axis=-1).T
    sign = np.where(np.arange(HEAD) < HEAD // 2, -1.0, 1.0)[:, None]
    down = 2.0 ** -LOG_V
    trig = np.stack([np.tile(np.cos(emb) * down, (4, 1)), np.tile(np.sin(emb) * sign * down, (4, 1))], axis=1).astype(np.float32)
    small = np.concatenate([np.tile(E - np.arange(E), J), np.arange(E) * T, np.arange(NTILE)]).astype(np.float32)
    arrays = {
        "x": x,
        "w_all": np.ascontiguousarray(np.stack([chunks(w) for w in mats])),
        "gate": np.ascontiguousarray(chunks(a["L0_ffn_gate_w"])),
        "bias": a["L0_ffn_expert_b"],
        "trig": trig,
        "small": np.tile(small, (P, 1)),
    }
    nc = bacc.Bacc("TRN2", target_bir_lowering=False, num_devices=1)
    args = [nc.dram_tensor(n, v.shape, mybir.dt.from_np(v.dtype), kind="ExternalInput").ap() for n, v in arrays.items()]
    out = nc.dram_tensor("out", x.shape, F32, kind="ExternalOutput").ap()
    moe_attention_layer(nc, *args, out)
    r = run_bass_kernel_spmd(nc, [arrays], core_ids=[0])
    return r.results[0]["out"]
```

```python
import numpy as np

import concourse.bass as bass
from concourse import mybir

F32 = mybir.dt.float32
F16 = mybir.dt.float16
BF16 = mybir.dt.bfloat16
I32 = mybir.dt.int32
ALU = mybir.AluOpType
ACT = mybir.ActivationFunctionType
AX = mybir.AxisListType

P = 128
EXP_ONE = 1 << 23
EPS = 1e-5
LOG_X = 11
LOG_W = 14
LOG_V = 20
MASKED = -3.0e38


class Steps:

    def __init__(self, engine, sem):
        self.engine, self.sem, self.n, self.before = engine, sem, 0, 0

    def link(self, ins, wait=None):
        self.n += 1
        ins.then_inc(self.sem, 1)
        (wait or type(self.engine).wait_ge)(self.engine, self.sem, self.before + self.n)

    def enter(self, per_turn):
        self.outside, self.per_turn = self.n, per_turn

    def turn(self, i):
        self.n, self.before = 0, self.outside + i * self.per_turn

    def leave(self, turns):
        assert self.n == self.per_turn, (self.n, self.per_turn)
        self.n, self.before = self.outside + turns * self.per_turn, 0


def moe_attention_layer(nc, x, w_all, gate, bias, trig, small, out):
    B, S, D = x.shape
    NM = w_all.shape[0]
    E = gate.shape[2]
    NQ = NM - E
    C = D // P
    J = S // P
    T = B * S
    NT = T // P
    NTILE = -(-(2 * NT + E - 1) // 4) * 4
    NCOL = E * NT + 8
    HG = 4
    G = D // P
    HD = P // HG
    N = B * G
    x_v = x.rearrange("b (j p) d -> b p j d", p=P)
    x_t = x.rearrange("b (j p) d -> (b j) p d", p=P)
    out_t = out.rearrange("b (j p) d -> (b j) p d", p=P)

    xn_rows = nc.dram_tensor("xn_rows", (T, 2 * D), F16, kind="Internal").ap()
    slot_table = nc.dram_tensor("slot_table", (P * NCOL, 1), I32, kind="Internal").ap()
    qk_rows = nc.dram_tensor("qk_rows", (2, 2, P, 2, S), F16, kind="Internal").ap()
    y_rows = nc.dram_tensor("y_rows", (NTILE * P, D), F32, kind="Internal").ap()

    place = [nc.sbuf_base + 127 & ~127]

    def at(name, shape, dtype, offset=None):
        size = int(np.prod(shape[1:])) * (2 if dtype in (F16, BF16) else 4)
        o = place[0] if offset is None else offset
        t = nc.alloc_sbuf_tensor_at(name, shape, dtype, offset=o)
        place[0] = o + (size + 31 & ~31)
        return t

    ident16 = at("ident16", [P, P], F16)
    before16 = at("before16", [P, P], F16)
    ones16 = at("ones16", [P, P], F16)
    ident32 = at("ident32", [P, P], F32)
    causal = at("causal", [P, P], BF16)
    small_sb = at("small_sb", [P, small.shape[1]], F32)
    prefer = small_sb[:, 0:J * E].rearrange("p (j e) -> p j e", j=J)
    first_row = small_sb[:, J * E:J * E + E]
    tile_no = small_sb[:, J * E + E:J * E + E + NTILE]
    slots = at("slots", [P, 2, NT], I32)
    gap = at("gap", [P, NT], F32)
    w12 = at("w12", [P, 2, NT], F32)
    amax = at("amax", [P, 16], F32)
    amax_all = at("amax_all", [P, 16], F32)
    expo = at("expo", [P, 16], I32)
    up = at("up", [P, 16], I32)
    down = at("down", [P, 16], I32)
    factors = at("factors", [P, 3], F32)
    gate_hl = at("gate_hl", [P, C, 2 * E], F16)
    gate_f = at("gate_f", [P, C, E], F32)
    carry = at("carry", [P, E], F32)
    token_no = [at(f"token_no{u}", [P, J], I32) for u in range(2)]
    target = [at(f"target{u}", [P, 2, J], I32) for u in range(2)]
    xT = at("xT", [P, 2 * C, T], F16)
    end_common = place[0]
    w_exp = at("w_exp", [P, E, 2, C, D], F16)
    after_exp = place[0]

    x_in = [at(f"x_in{u}", [P, J, D], F32) for u in range(2)]
    x_n = at("x_n", [P, J, D], F32)
    x_hl = [at(f"x_hl{u}", [P, J, 2, D], F16) for u in range(2)]
    w_in = [at(f"w_in{u}", [P, C, D], F32) for u in range(2)]
    zero_i = at("zero_i", [P, NCOL], I32)
    stats = at("stats", [P, J, 6], F32)
    mean_var = at("mean_var", [P, J, 2], F32)
    var_eps = at("var_eps", [P, J], F32)
    std = at("std", [P, J], F32)
    r0 = at("r0", [P, J], F32)
    r1 = at("r1", [P, J], F32)
    rstd = at("rstd", [P, J], F32)
    logit = at("logit", [P, J, E], F32)
    rest = at("rest", [P, J, E], F32)
    best = at("best", [P, 2, J], F32)
    same = at("same", [P, J, E], F32)
    rank = at("rank", [P, J], F32)
    one_hot = [at(f"one_hot{k}", [P, J, E], F32) for k in range(2)]
    chosen = at("chosen", [P, J * E], F16)
    place_f = at("place_f", [P, J, E], F32)
    picked = at("picked", [P, 2, J, E], F32)
    slot_f = at("slot_f", [P, 2, J], F32)
    low7 = at("low7", [P, 2, J], I32)
    high = at("high", [P, 2, J], I32)

    place[0] = after_exp
    w_att = at("w_att", [P, NQ, 2, C, D], F16)
    bias_all = at("bias_all", [P, E, D], F32)
    moe0 = place[0]
    wq_in = [at(f"wq_in{u}", [P, C, D], F32) for u in range(2)]
    place[0] = moe0
    x_g = [at(f"x_g{u}", [P, 2 * D], F16) for u in range(4)]
    x_gT = [at(f"x_gT{u}", [P, 2 * C, P], F16) for u in range(2)]
    y_sb = [at(f"y_sb{u}", [P, D], F32) for u in range(4)]
    idx = [at(f"idx{u}", [P, 1], I32) for u in range(4)]
    tok_of = at("tok_of", [P, NCOL], I32)
    slot_e = at("slot_e", [P, 2, NT], F32)
    slot_i = at("slot_i", [P, 2, NT], I32)
    slot_now = at("slot_now", [P, 2, NT], F32)
    move = at("move", [P, 2, NT], F32)
    moves = at("moves", [P, E], F32)
    exp_col = at("exp_col", [P, 2, NTILE], I32)
    cnt_i = at("cnt_i", [P, E], I32)
    tiles = at("tiles", [P, E], F32)
    ends = at("ends", [P, 2, E], F32)
    past = at("past", [P, NTILE, E], F32)
    n_past = at("n_past", [P, NTILE], F32)
    t_past = at("t_past", [P, NTILE], F32)
    t_col = at("t_col", [P, NTILE], F32)

    place[0] = end_common
    pT = at("pT", [P, HG, J, S], F32)
    o_hl = [at(f"o_hl{u}", [P, G, 2, S], F16) for u in range(2)]
    q_stack = [at(f"q_stack{u}", [P, HG, S], F16) for u in range(2)]
    k_stack = [at(f"k_stack{u}", [P, HG, S], F16) for u in range(2)]
    assert place[0] <= after_exp
    place[0] = moe0 - 4 * E * D
    trig_sb = at("trig_sb", [P, 2, S], F32)
    plain = [at(f"plain_{n}", [P, S], F32) for n in "qk"]
    turned = [at(f"turned_{n}", [P, S], F32) for n in "qk"]
    qk_hl = [at(f"{n}_hl", [P, 2, S], F16) for n in "qk"]
    v_sb = [at(f"v_sb{u}", [P, J, P], F32) for u in range(2)]
    p_sb = [at(f"p_sb{u}", [P, 2, S], F32) for u in range(2)]
    o_sb = at("o_sb", [P, S], F32)
    sum_sb = [at(f"sum_sb{u}", [P, D], F32) for u in range(2)]
    y_in = [at(f"y_in{u}", [P, 2, D], F32) for u in range(2)]
    idx_y = [at(f"idx_y{u}", [P, 2], I32) for u in range(2)]
    top = at("top", [P, 2, 2], F32)
    shift = at("shift", [P, 2, 2], F32)
    den = [at(f"den{u}", [P, J, HG], F32) for u in range(2)]
    rden = at("rden", [P, J, HG, 1], F32)
    rden_wide = at("rden_wide", [P, J, HG, HD], F32)

    psum = nc.alloc_psum_tensor("psum", [P, 8, 512], F32)
    banks = [psum[:, i, :] for i in range(8)]

    def s_banks(u):
        return psum[:, BANK_S + 2 * u:BANK_S + 2 * u + 2, :]

    def half(bank):
        return banks[bank].bitcast(F16)

    def sem(name):
        return nc.alloc_semaphore(name)

    const_in, gate_in, table_zero = sem("const_in"), sem("gate_in"), sem("table_zero")
    x_loaded = [sem("x_loaded0"), sem("x_loaded1")]
    w_loaded = [sem("w_loaded0"), sem("w_loaded1")]
    xn_stored = [sem("xn_stored0"), sem("xn_stored1")]
    dve_own, pool_own = sem("dve_own"), sem("pool_own")
    consts_made = sem("consts_made")
    amax_done, amax_everywhere, scale_done = sem("amax_done"), sem("amax_everywhere"), sem("scale_done")
    w_hi_done, w_lo_done = sem("w_hi_done"), sem("w_lo_done")
    var_done, std_done, xn_done, x_hi_done, x_lo_done = (sem(n) for n in ("var_done", "std_done", "xn_done", "x_hi_done", "x_lo_done"))
    xt_done, xT_copied, gate_done, logit_read = (sem(n) for n in ("xt_done", "xT_copied", "gate_done", "logit_read"))
    chosen_done, rank_done, rank_read, target_done = (sem(n) for n in ("chosen_done", "rank_done", "rank_read", "target_done"))
    scattered = [sem("scattered0"), sem("scattered1")]
    gap_done, gap_exp, w12_done, tiles_done, table_loaded, bias_loaded = (sem(n) for n in ("gap_done", "gap_exp", "w12_done", "tiles_done", "table_loaded", "bias_loaded"))
    slots_final = sem("slots_final")
    gathered = [sem(f"gathered{u}") for u in range(4)]
    xg_turned, xgT_copied, y_done, y_scaled = (sem(n) for n in ("xg_turned", "xgT_copied", "y_done", "y_scaled"))
    y_stored = [sem(f"y_stored{u}") for u in range(4)]
    waited_apart = sem("waited_apart")
    trig_in, qk_summed, qk_rotated, qk_roped, qk_hi, qk_lo = (sem(n) for n in ("trig_in", "qk_summed", "qk_rotated", "qk_roped", "qk_hi", "qk_lo"))
    q_stacked = [sem(f"q_stacked{u}") for u in range(2)]
    k_stacked = [sem(f"k_stacked{u}") for u in range(2)]
    v_summed, v_read, factors_done = sem("v_summed"), sem("v_read"), sem("factors_done")
    scores_done, shift_done, exp_done, pt_turned = (sem(n) for n in ("scores_done", "shift_done", "exp_done", "pt_turned"))
    pt_copied = [sem(f"pt_copied{u}") for u in range(2)]
    rden_done, pv_done, o_read, o_hi, o_lo = (sem(n) for n in ("rden_done", "pv_done", "o_read", "o_hi", "o_lo"))
    wo_done, sum_done = sem("wo_done"), sem("sum_done")
    x_again = [sem(f"x_again{u}") for u in range(2)]
    qk_stored = [sem("q_stored"), sem("k_stored")]
    y_back = [sem(f"y_back{u}") for u in range(2)]
    out_stored = [sem(f"out_stored{u}") for u in range(2)]

    BANK_XT, BANK_GATE, BANK_RANK = 0, 4, 6

    def scale_ops(dve, own, m, at=None):
        own.link(dve.tensor_scalar(expo[:, m].bitcast(F32), amax_all[:, m if at is None else at], 2.0 ** -60, None, ALU.max))
        own.link(dve.tensor_scalar(expo[:, m], expo[:, m], 0x7F800000, None, ALU.bitwise_and))
        own.link(dve.tensor_scalar(up[:, m], expo[:, m], -1.0, float((254 + LOG_W) * EXP_ONE), ALU.mult, ALU.add))
        return dve.tensor_scalar(down[:, m], expo[:, m], float(-(LOG_W + LOG_X) * EXP_ONE), None, ALU.add)

    def wait_apart(engine, on, value):
        engine.wait_ge(on, value)
        engine.sem_inc(waited_apart, 1)

    def fresh(engine, value):
        r = engine.alloc_register()
        engine.reg_mov(r, value)
        return engine.snap(r, min_val=1, max_val=B - 2)

    GM = NM

    BANK_S, BANK_PT, BANK_MISC = 0, 4, 6
    BANK_Q, BANK_O = BANK_MISC, BANK_MISC + 1

    UNITS = 2 * J
    PT_FILLS = 13
    FILL_R = 3

    def fill(n, a):
        return PT_FILLS * n + a - 3

    def fills(k, first=False):
        if first and k == 0:
            return (FILL_R,)
        return {7: (0, 1), 0: (2,), 1: (4,), 2: (5,), 3: (6,), 4: (7, 8), 5: (9, 10), 6: (11, 12)}[k]

    def fill_r(b):
        return 2 if isinstance(b, int) and b == B else FILL_R

    def is_first(b, g):
        return g == 0 and isinstance(b, int) and b == 0

    def pt_bank(g, a):
        return (PT_FILLS * g + a - 3) % 2

    def fills_up_to(bank, b, g, a):
        return b * (G * PT_FILLS // 2) + (PT_FILLS * g + a - 3 - bank) // 2 + 1

    def two_on(b, g):
        if g + 2 < G:
            return b, g + 2
        return None if isinstance(b, int) and b == B - 1 else (b + 1, g + 2 - G)

    def part(k, a):
        i, pair = k // 2, k % 2
        n = i + 1
        if len(fills(k)) == 1:
            return ([(2 * pair + h, j, (h * n + j) * P) for h in range(2) for j in range(n)],
                    lambda bank: bank[:, 0:2 * n * P].rearrange("p (h j t) -> p h j t", h=2, j=n),
                    pT[:, 2 * pair:2 * pair + 2, 0:n, i * P:(i + 1) * P])
        h = 2 * pair + fills(k).index(a)
        return ([(h, j, j * P) for j in range(n)],
                lambda bank: bank[:, 0:n * P].rearrange("p (j t) -> p j t", j=n),
                pT[:, h, 0:n, i * P:(i + 1) * P])

    block = nc.Block()
    with block:
        @block.sync
        def _(sp):
            sp.dma_start(small_sb[:], small).then_inc(const_in, 16)
            sp.dma_start(gate_f[:], gate).then_inc(gate_in, 16)

            def load(b, u, first=False):
                if not first:
                    sp.wait_ge(xn_done, b - 1)
                sp.dma_start(x_in[u][:], x_v[bass.ds(b, 1)].rearrange("b p j d -> p (b j) d")).then_inc(x_loaded[u], 16)
                if not first:
                    sp.wait_ge(w_lo_done, b)
                sp.dma_start(w_in[u][:], w_all[bass.ds(b, 1)].rearrange("b p c d -> p (b c) d")).then_inc(w_loaded[u], 16)

            def store(b, u):
                sp.wait_ge(x_hi_done, b + 1)
                sp.wait_ge(x_lo_done, b + 1)
                sp.dma_start(xn_rows[bass.ds(b * S, S), :].rearrange("(j p) c -> p j c", p=P),
                             x_hl[u][:].rearrange("p j h d -> p j (h d)")).then_inc(xn_stored[u], 16)

            load(0, 0, True)
            load(1, 1, True)
            sp.wait_ge(consts_made, 1)
            sp.dma_start(slot_table.rearrange("(p c) o -> p (c o)", p=P), zero_i[:]).then_inc(table_zero, 16)
            with sp.Fori(0, B // 2 - 1) as i:
                for u in range(2):
                    store(2 * i + u, u)
                    load(2 * i + 2 + u, u)
            for u in range(2):
                store(B - 2 + u, u)

            sp.wait_ge(w_lo_done, E + 1)
            sp.wait_ge(xt_done, NT)
            sp.wait_ge(target_done, B)
            for u in range(2):
                sp.wait_ge(xn_stored[u], 16 * (B // 2))
            sp.dma_start(bias_all[:], bias.unsqueeze(0).broadcast_to([P, E, D])).then_inc(bias_loaded, 16)
            for m in range(NQ):
                if m >= 2:
                    sp.wait_ge(w_lo_done, E + m)
                sp.dma_start(wq_in[m % 2][:], w_all[E + m]).then_inc(w_loaded[m % 2], 16)
            for u in range(2):
                sp.wait_ge(scattered[u], 16 * J * B)
            sp.dma_start(tok_of[:], slot_table.rearrange("(p c) o -> p (c o)", p=P)).then_inc(table_loaded, 16)
            sp.wait_ge(tiles_done, 1)

            def store_y(s, u):
                sp.wait_ge(y_scaled, s + 1)
                sp.dma_start(y_rows[bass.ds(s * P, P), :], y_sb[u][:]).then_inc(y_stored[u], 16)

            with sp.Fori(0, NTILE // 4) as i:
                for u in range(4):
                    store_y(4 * i + u, u)
            for u in range(4):
                sp.wait_ge(y_stored[u], 16 * (NTILE // 4))

            sp.wait_ge(y_scaled, NTILE)
            sp.dma_start(trig_sb[:], trig).then_inc(trig_in, 16)
            sp.wait_ge(y_done, NTILE)

            def store_qk(what, b, g, first=False):
                n, u = G * b + g, g % 2
                wait_apart(sp, qk_lo, 2 * n + what + 1)
                if not first:
                    wait_apart(sp, (q_stacked, k_stacked)[what][u], 16 * 4 * (b * (G // 2) + g // 2))
                sp.dma_start(qk_rows[u, what], qk_hl[what][:]).then_inc(qk_stored[what], 16)

            def stack(what, b, g, first=False):
                stacks, done, order = ((q_stack, q_stacked, (0, 1, 0, 1)), (k_stack, k_stacked, (0, 0, 1, 1)))[what]
                n, u = G * b + g, g % 2
                wait_apart(sp, qk_stored[what], 16 * (n + 1))
                if not first:
                    wait_apart(sp, scores_done, UNITS * (n - 1))
                for place_no, half_no in enumerate(order):
                    sp.dma_start(stacks[u][place_no * HD:(place_no + 1) * HD, :, :],
                                 qk_rows[u, what].rearrange("(h p) f s -> f p h s", p=HD)[half_no]).then_inc(done[u], 16)

            def load_x(w, u):
                sp.dma_start(sum_sb[u][:], x_t[bass.ds(w, 1)].rearrange("w p d -> p (w d)")).then_inc(x_again[u], 16)

            def store_out(w, u, stores=None):
                sp.wait_ge(sum_done, w + 1)
                sp.dma_start(out_t[bass.ds(w, 1)].rearrange("w p d -> p (w d)"), sum_sb[u][:]).then_inc(out_stored[u], 16)
                if stores is not None:
                    wait_apart(sp, out_stored[u], 16 * stores)
                    load_x(w + 2, u)

            def attention_step(b, g, sums=True):
                ahead = two_on(b, g)
                if ahead:
                    for what in range(2):
                        store_qk(what, *ahead)
                if sums:
                    store_out(J * (b - 1) + g, g % 2, J // 2 * (b - 1) + g // 2 + 1)
                if ahead:
                    for what in range(2):
                        stack(what, *ahead)

            for g in range(2):
                for what in range(2):
                    store_qk(what, 0, g, True)
                    stack(what, 0, g, True)
            for g in range(G):
                attention_step(0, g, sums=False)
            for w in range(2):
                load_x(w, w)
            with sp.Fori(0, B // 2 - 1) as i:
                for u in range(2):
                    for g in range(G):
                        attention_step(2 * i + 1 + u, g)
            for g in range(G):
                attention_step(B - 1, g)
            for j in range(J):
                store_out(NT - J + j, j % 2, (NT - J + j) // 2 + 1 if j < J - 2 else None)
            for u in range(2):
                sp.wait_ge(out_stored[u], 16 * (NT // 2))

        @block.gpsimd
        def _(pool):
            own = Steps(pool, pool_own)
            own.link(pool.memset(zero_i[:], 0))
            own.link(pool.memset(ident16[:], 0.0))
            own.link(pool.memset(ident32[:], 0.0))
            own.link(pool.memset(ones16[:], 1.0))
            own.link(pool.memset(causal[:], 0.0))
            own.link(pool.affine_select(out=ident16[:], in_=ident16[:], compare_op=ALU.not_equal, fill=1.0,
                                        base=0, pattern=[[-1, P]], channel_multiplier=1))
            own.link(pool.affine_select(out=ident32[:], in_=ident32[:], compare_op=ALU.not_equal, fill=1.0,
                                        base=0, pattern=[[-1, P]], channel_multiplier=1))
            own.link(pool.affine_select(out=before16[:], in_=ones16[:], compare_op=ALU.is_gt, fill=0.0,
                                        base=0, pattern=[[1, P]], channel_multiplier=-1))
            own.link(pool.affine_select(out=causal[:], in_=causal[:], compare_op=ALU.is_ge, fill=MASKED,
                                        base=0, pattern=[[-1, P]], channel_multiplier=1))
            for u in range(2):
                last = pool.iota(token_no[u][:], [[P, J]], base=u * S, channel_multiplier=1)
                own.link(last) if u == 0 else last.then_inc(consts_made, 1)

            pool.wait_ge(amax_done, 1)
            pool.partition_all_reduce(amax_all[:, GM:GM + 1], amax[:, GM:GM + 1], P, bass.bass_isa.ReduceOp.max)\
                .then_inc(amax_everywhere, 1)

            def split(b, u):
                wait_apart(pool, amax_done, b + 2)
                pool.partition_all_reduce(amax_all[:, u:u + 1], amax[:, u:u + 1], P, bass.bass_isa.ReduceOp.max)\
                    .then_inc(amax_everywhere, 1)
                pool.wait_ge(x_hi_done, b + 1)
                pool.tensor_tensor(x_hl[u][:, :, 1, :], x_n[:], x_hl[u][:, :, 0, :], ALU.subtract).then_inc(x_lo_done, 1)

            def scatter(b, u, half_b):
                wait_apart(pool, target_done, b + 1)
                for j in range(J):
                    for k in range(2):
                        pool.indirect_dma_start(slot_table, bass.IndirectOffsetOnAxis(ap=target[u][:, k, j:j + 1], axis=0),
                                                token_no[u][:, j:j + 1], None).then_inc(scattered[u], 16)
                wait_apart(pool, scattered[u], 16 * 2 * J * (half_b + 1))
                own.link(pool.tensor_scalar(token_no[u][:], token_no[u][:], float(2 * S), None, ALU.add))

            split(0, 0)
            pool.wait_ge(table_zero, 16)
            own.enter(2)
            with pool.Fori(0, B // 2 - 1) as i:
                own.turn(i)
                split(2 * i + 1, 1)
                scatter(2 * i, 0, i)
                split(2 * i + 2, 0)
                scatter(2 * i + 1, 1, i)
            own.leave(B // 2 - 1)
            split(B - 1, 1)
            scatter(B - 2, 0, B // 2 - 1)
            scatter(B - 1, 1, B // 2 - 1)

            for m in range(E, NM):
                pool.wait_ge(amax_done, m + 2)
                pool.partition_all_reduce(amax_all[:, m:m + 1], amax[:, m:m + 1], P, bass.bass_isa.ReduceOp.max)\
                    .then_inc(amax_everywhere, 1)

            pool.wait_ge(table_loaded, 16)
            pool.wait_ge(tiles_done, 1)
            pool.wait_ge(w_lo_done, NM + 1)

            def gather(s, u, turn, first=False):
                col = pool.value_load(exp_col[0:1, 1, bass.ds(s, 1)], min_val=0, max_val=NCOL - 1)
                if not first:
                    pool.wait_ge(gathered[u], 16 * turn)
                    pool.wait_ge(xg_turned, s - 3)
                own.link(pool.tensor_copy(idx[u][:], tok_of[:, bass.ds(col, 1)]), wait_apart)
                pool.indirect_dma_start(x_g[u][:], None, xn_rows, bass.IndirectOffsetOnAxis(ap=idx[u][:], axis=0))\
                    .then_inc(gathered[u], 16)

            for u in range(4):
                gather(u, u, 0, True)
            own.enter(4)
            with pool.Fori(1, NTILE // 4) as i:
                own.turn(i - 1)
                for u in range(4):
                    gather(4 * i + u, u, i)
            own.leave(NTILE // 4 - 1)

            def rope(what, n):
                w = 2 * n + what
                pool.wait_ge(qk_rotated, w + 1)
                own.link(pool.tensor_tensor(turned[what][:], turned[what][:], trig_sb[:, 1, :], ALU.mult))
                pool.tensor_tensor(plain[what][:], plain[what][:], turned[what][:], ALU.add).then_inc(qk_roped, 1)

            def low_qk(what, n):
                pool.wait_ge(qk_hi, 2 * n + what + 1)
                pool.tensor_tensor(qk_hl[what][:, 1, :], plain[what][:], qk_hl[what][:, 0, :], ALU.subtract).then_inc(qk_lo, 1)

            def low_o(n, u, g):
                pool.wait_ge(o_hi, n + 1)
                pool.tensor_tensor(o_hl[u][:, g, 1, :], o_sb[:], o_hl[u][:, g, 0, :], ALU.subtract).then_inc(o_lo, 1)

            def gather_y(w, u, first=False):
                if not first:
                    pool.wait_ge(sum_done, w - 1)
                own.link(pool.tensor_copy(idx_y[u][:], slots[:, :, bass.ds(w, 1)].rearrange("p k w -> p (k w)")), wait_apart)
                for k in range(2):
                    pool.indirect_dma_start(y_in[u][:, k, :], None, y_rows, bass.IndirectOffsetOnAxis(ap=idx_y[u][:, k:k + 1], axis=0))\
                        .then_inc(y_back[u], 16)

            def attention_step(b, u, g, prev=True, sums=True):
                n, ahead = G * b + g, two_on(b, g)
                if ahead:
                    rope(0, n + 2)
                if prev:
                    low_o(n - 1, u if g else 1 - u, (g - 1) % G)
                if ahead:
                    low_qk(0, n + 2)
                    rope(1, n + 2)
                    low_qk(1, n + 2)
                if sums:
                    gather_y(J * (b - 1) + g + 2, g % 2)

            pool.wait_ge(trig_in, 16)
            pool.wait_ge(slots_final, 1)
            for u in range(4):
                pool.wait_ge(y_stored[u], 16 * (NTILE // 4))
            for n in range(2):
                for what in range(2):
                    rope(what, n)
                    low_qk(what, n)
            for g in range(G):
                attention_step(0, 0, g, prev=g > 0, sums=False)
            for w in range(2):
                gather_y(w, w, True)
            own.enter(2 * (2 * G + J))
            with pool.Fori(0, B // 2 - 1) as i:
                own.turn(i)
                for u in range(2):
                    for g in range(G):
                        attention_step(2 * i + 1 + u, 1 - u, g)
            own.leave(B // 2 - 1)
            for g in range(G):
                attention_step(B - 1, 1, g)
            low_o(N - 1, 1, G - 1)
            for j in range(2, J):
                gather_y(NT - J + j, j % 2)

        @block.scalar
        def _(act):
            act.wait_ge(scale_done, 1)
            act.activation(gate_hl[:, :, 0:E], gate_f[:], ACT.Identity, scale=up[:, GM:GM + 1].bitcast(F32)).then_inc(w_hi_done, 1)

            def batch(b, u, half_b, first=False):
                act.wait_ge(var_done, b + 1)
                act.activation(std[:], var_eps[:], ACT.Sqrt).then_inc(std_done, 1)
                act.wait_ge(xn_done, b + 1)
                if not first:
                    act.wait_ge(xn_stored[u], 16 * half_b)
                    act.wait_ge(xt_done, J * (b - 1))
                act.activation(x_hl[u][:, :, 0, :], x_n[:], ACT.Copy).then_inc(x_hi_done, 1)
                act.wait_ge(scale_done, b + 2)
                act.activation(w_exp[:, bass.ds(b, 1), 0, :, :].rearrange("p m c d -> p (m c) d"), w_in[u][:], ACT.Identity,
                               scale=up[:, bass.ds(b, 1)].bitcast(F32)).then_inc(w_hi_done, 1)
                for j in range(J):
                    act.wait_ge(xt_done, J * b + j + 1)
                    act.activation(xT[:, :, bass.ds(b * S + j * P, P)],
                                   half(BANK_XT + j).rearrange("p (c t) -> p c t", t=P), ACT.Copy).then_inc(xT_copied, 1)

            batch(0, 0, 0, True)
            batch(1, 1, 0, True)
            with act.Fori(1, B // 2) as i:
                for u in range(2):
                    batch(2 * i + u, u, i)

            act.wait_ge(gap_done, B)
            act.activation(w12[:, 1, :], gap[:], ACT.Exp, scale=down[:, GM:GM + 1].bitcast(F32)).then_inc(gap_exp, 1)
            act.wait_ge(bias_loaded, 16)
            for m in range(E, NM):
                act.wait_ge(scale_done, m + 2)
                act.activation(w_att[:, m - E, 0, :, :], wq_in[m % 2][:], ACT.Identity,
                               scale=up[:, m:m + 1].bitcast(F32)).then_inc(w_hi_done, 1)

            def copy_xgT(s, u, first=False):
                act.wait_ge(xg_turned, s + 1)
                if not first:
                    act.wait_ge(y_done, s - 1)
                act.activation(x_gT[u][:], half(u).rearrange("p (c t) -> p c t", t=P), ACT.Copy).then_inc(xgT_copied, 1)

            act.wait_ge(w_lo_done, NM + 1)
            for u in range(2):
                copy_xgT(u, u, True)
            with act.Fori(1, NTILE // 2) as i:
                for u in range(2):
                    copy_xgT(2 * i + u, u)

            def high_qk(what, n, first=False):
                act.wait_ge(qk_roped, 2 * n + what + 1)
                if not first:
                    act.wait_ge(qk_stored[what], 16 * n)
                act.activation(qk_hl[what][:, 0, :], plain[what][:], ACT.Copy).then_inc(qk_hi, 1)

            def take_v(n, g, prev):
                act.wait_ge(v_summed, n + 1)
                if prev:
                    act.wait_ge(pv_done, n - 1)
                act.activation(v_sb[g % 2][:], banks[BANK_O][:].rearrange("p (j d) -> p j d", j=J), ACT.Copy,
                               scale=2.0 ** -LOG_V).then_inc(v_read, 1)

            def exps(b, g, k, free=True):
                n, i, pair = G * b + g, k // 2, k % 2
                W = (i + 1) * P
                act.wait_ge(shift_done, UNITS * n + k + 1)
                if free:
                    act.wait_ge(pt_turned, (fill(n, fills(k - 2, is_first(b, g))[-1]) if k >= 2 else fill(n, fills(7)[-1]) if k == 1
                                            else fill(n - 1, fills(6)[-1])) + 1)
                for h in range(2):
                    last = act.activation(p_sb[k % 2][:, h, 0:W], banks[BANK_S + 2 * (k % 2) + h][:, 0:W], ACT.Exp,
                                          bias=shift[:, k % 2, h:h + 1], scale=factors[:, 0:1],
                                          accum_out=den[g % 2][:, i, 2 * pair + h:2 * pair + h + 1])
                last.then_inc(exp_done, 1)

            def copy_pt(b, g, k, a):
                n = G * b + g
                bank = pt_bank(g, a)
                act.wait_ge(pt_turned, fill(n, a) + 1)
                _, view, to = part(k, a)
                act.activation(to, view(banks[BANK_PT + bank]), ACT.Copy).then_inc(pt_copied[bank], 1)

            def high_o(n, u, g):
                act.activation(o_hl[u][:, g, 0, :], o_sb[:], ACT.Copy).then_inc(o_hi, 1)

            def attention_step(b, u, g, prev=True, nxt=True):
                n = G * b + g
                exps(b, g, 0, prev)
                if prev:
                    copy_pt(b, g, 7, 1)
                exps(b, g, 1, prev)
                exps(b, g, 2)
                if prev:
                    bank = pt_bank(g, fill_r(b))
                    act.wait_ge(pt_turned, fill(n, fill_r(b)) + 1)
                    if not (isinstance(n, int) and n == 1):
                        act.wait_ge(o_lo, n - 1)
                    act.activation(o_sb[:], banks[BANK_PT + bank][:], ACT.Copy).then_inc(pt_copied[bank], 1)
                    act.wait_ge(o_read, n)
                    if g == 1 and not (isinstance(b, int) and b < 2):
                        act.wait_ge(wo_done, J * (b - 1))
                    high_o(n - 1, u if g else 1 - u, (g - 1) % G)
                exps(b, g, 3)
                if two_on(b, g):
                    high_qk(0, n + 2)
                exps(b, g, 4)
                if prev:
                    act.wait_ge(pv_done, n)
                copy_pt(b, g, 3, 6)
                exps(b, g, 5)
                if two_on(b, g):
                    high_qk(1, n + 2)
                copy_pt(b, g, 4, 8)
                exps(b, g, 6)
                copy_pt(b, g, 5, 10)
                exps(b, g, 7)
                copy_pt(b, g, 6, 12)
                if nxt:
                    take_v(n + 1, g + 1, prev)

            act.wait_ge(y_scaled, NTILE)
            for n in range(2):
                for what in range(2):
                    high_qk(what, n, n == 0)
            take_v(0, 0, False)
            act.wait_ge(factors_done, 1)
            for g in range(G):
                attention_step(0, 0, g, prev=g > 0)
            with act.Fori(0, B // 2 - 1) as i:
                for u in range(2):
                    for g in range(G):
                        attention_step(2 * i + 1 + u, 1 - u, g)
            for g in range(G):
                attention_step(B - 1, 1, g, nxt=g < G - 1)
            copy_pt(B, 0, 7, 1)
            bank = pt_bank(0, fill_r(B))
            act.wait_ge(pt_turned, fill(N, fill_r(B)) + 1)
            act.wait_ge(o_lo, N - 1)
            act.activation(o_sb[:], banks[BANK_PT + bank][:], ACT.Copy).then_inc(pt_copied[bank], 1)
            act.wait_ge(o_read, N)
            high_o(N - 1, 1, G - 1)

        @block.tensor
        def _(pe):
            pe.wait_ge(consts_made, 1)

            def ranks(b, v, first=False):
                bank = banks[BANK_RANK + v]
                pe.wait_ge(chosen_done, b + 1)
                if not first:
                    pe.wait_ge(rank_read, b - 1)
                for j in range(J + 1):
                    o = bank[:, j * E:(j + 1) * E]
                    for k in range(j + (j < J)):
                        now = pe.matmul(o, before16[:] if k == j else ones16[:], chosen[:, k * E:(k + 1) * E],
                                        start=k == 0, stop=k == min(j, J - 1))
                now.then_inc(rank_done, 1)

            def turn_x(b, u, first=False):
                pe.wait_ge(x_lo_done, b + 1)
                for j in range(J):
                    if not first:
                        pe.wait_ge(xT_copied, J * (b - 1) + j + 1)
                    for c in range(2 * C):
                        now = pe.transpose(half(BANK_XT + j)[:, c * P:(c + 1) * P],
                                           x_hl[u][:, j, c // C, c % C * P:(c % C + 1) * P], ident16[:])
                    now.then_inc(xt_done, 1)

            def gate_logits(b, v, first=False):
                bank = banks[BANK_GATE + v]
                pe.wait_ge(xT_copied, J * (b + 1))
                if not first:
                    pe.wait_ge(logit_read, b - 1)
                for j in range(J):
                    toks = bass.ds(b * S + j * P, P)
                    o = bank[:, j * 2 * E:(j + 1) * 2 * E]
                    pe.matmul(o, xT[:, 0, toks], gate_hl[:, 0, :], start=True, stop=False)
                    for c in range(C):
                        pe.matmul(o[:, 0:E], xT[:, C + c, toks], gate_hl[:, c, 0:E], start=False, stop=False)
                    for c in range(1, C):
                        now = pe.matmul(o, xT[:, c, toks], gate_hl[:, c, :], start=False, stop=c == C - 1)
                now.then_inc(gate_done, 1)

            turn_x(0, 0, True)
            pe.wait_ge(w_lo_done, 1)
            gate_logits(0, 0, True)
            ranks(0, 0, True)
            turn_x(1, 1)
            gate_logits(1, 1, True)
            ranks(1, 1, True)
            turn_x(2, 0)
            gate_logits(2, 0)
            with pe.Fori(1, B // 2 - 1) as i:
                for v in range(2):
                    ranks(2 * i + v, v)
                    turn_x(2 * i + v + 1, 1 - v)
                    gate_logits(2 * i + v + 1, 1 - v)
            ranks(B - 2, 0)
            turn_x(B - 1, 1)
            gate_logits(B - 1, 1)
            ranks(B - 1, 1)

            def turn_xg(s, u4, u2, turn, first=False):
                pe.wait_ge(gathered[u4], 16 * (turn + 1))
                if not first:
                    pe.wait_ge(xgT_copied, s - 1)
                for c in range(2 * C):
                    now = pe.transpose(half(u2)[:, c * P:(c + 1) * P], x_g[u4][:, c * P:(c + 1) * P], ident16[:])
                now.then_inc(xg_turned, 1)

            def expert(s, u, first=False):
                e = pe.value_load(exp_col[0:1, 0, bass.ds(s, 1)], min_val=0, max_val=E - 1)
                pe.wait_ge(xgT_copied, s + 1)
                if not first:
                    pe.wait_ge(y_scaled, s - 1)
                n = 0
                for c in range(C):
                    for xp, wp in ((0, 0), (0, 1), (1, 0)):
                        now = pe.matmul(banks[4 + u][:], x_gT[u][:, xp * C + c, :],
                                        w_exp[:, bass.ds(e, 1), wp, c, :].rearrange("p e d -> p (e d)"),
                                        start=n == 0, stop=n == 3 * C - 1)
                        n += 1
                now.then_inc(y_done, 1)

            pe.wait_ge(tiles_done, 1)
            pe.wait_ge(w_lo_done, NM + 1)
            turn_xg(0, 0, 0, 0, True)
            for s in range(4):
                turn_xg(s + 1, (s + 1) % 4, (s + 1) % 2, (s + 1) // 4, s == 0)
                expert(s, s % 2, s < 2)
            with pe.Fori(1, NTILE // 4 - 1) as i:
                for u in range(4):
                    turn_xg(4 * i + u + 1, (u + 1) % 4, (u + 1) % 2, i + (u + 1) // 4)
                    expert(4 * i + u, u % 2)
            for s in range(NTILE - 4, NTILE):
                if s + 1 < NTILE:
                    turn_xg(s + 1, (s + 1) % 4, (s + 1) % 2, (s + 1) // 4)
                expert(s, s % 2)

            def scores(b, g, k, free=True):
                n, i, pair = G * b + g, k // 2, k % 2
                W = (i + 1) * P
                if free:
                    pe.wait_ge(exp_done, UNITS * n + k - 1)
                for h in range(2):
                    o, head = banks[BANK_S + 2 * (k % 2) + h], 2 * pair + h
                    pe.matmul(o[:, 0:W], q_stack[g % 2][:, head, i * P:(i + 1) * P], k_stack[g % 2][:, head, 0:W],
                              start=True, stop=False)
                    last = pe.matmul(o[:, W - P:W], ident16[:], causal[:], start=False, stop=True)
                last.then_inc(scores_done, 1)

            def turn_p(b, g, k):
                n = G * b + g
                pe.wait_ge(exp_done, UNITS * (n - 1 if k == 7 else n) + k + 1)
                for a in fills(k, is_first(b, g)):
                    bank = pt_bank(g, a)
                    wait = fills_up_to(bank, b, g, a) - 1
                    if not isinstance(wait, int) or wait > 0:
                        pe.wait_ge(pt_copied[bank], wait)
                    blocks, _, _ = part(k, a)
                    for head, j, col in blocks:
                        last = pe.transpose(banks[BANK_PT + bank][:, col:col + P], p_sb[k % 2][:, head % 2, j * P:(j + 1) * P], ident32[:])
                    last.then_inc(pt_turned, 1)

            def times_v(b, g, nxt=True):
                n = G * b + g
                for bank in range(2):
                    pe.wait_ge(pt_copied[bank], fills_up_to(bank, b, g, 1))
                pe.wait_ge(v_read, n + 1 if nxt else n)
                for j in range(J):
                    for h in range(HG):
                        last = pe.matmul(banks[BANK_O][h * HD:(h + 1) * HD, j * P:S], v_sb[(g - 1) % 2][:, j, h * HD:(h + 1) * HD],
                                         pT[:, h, j, j * P:S], start=j == 0, stop=j == J - 1)
                last.then_inc(pv_done, 1)
                bank = pt_bank(g, fill_r(b))
                pe.wait_ge(rden_done, n)
                pe.wait_ge(pt_copied[bank], fills_up_to(bank, b, g, fill_r(b)) - 1)
                for i in range(J):
                    last = pe.transpose(banks[BANK_PT + bank][:, i * P:(i + 1) * P],
                                        rden_wide[:, i].rearrange("p h d -> p (h d)"), ident32[:])
                last.then_inc(pt_turned, 1)

            PASSES = ((0, 0), (0, 1), (1, 0))

            def project_qk(what, b, g, free):
                pieces = []
                for c in range(C):
                    for m, (xp, wp) in enumerate(PASSES):
                        def piece(c=c, m=m, xp=xp, wp=wp):
                            if c == 0 and m == 0 and free:
                                for s_, v_ in free:
                                    pe.wait_ge(s_, v_)
                            now = pe.matmul(banks[BANK_Q][:], w_att[:, what, wp, c, g * P:(g + 1) * P],
                                            xT[:, xp * C + c, bass.ds(b * S, S)],
                                            start=c == 0 and m == 0, stop=c == C - 1 and m == 2)
                            if c == C - 1 and m == 2:
                                now.then_inc(qk_summed, 1)
                        pieces.append(piece)
                return pieces

            def project_v(b, g, free):
                pieces = []
                for j in range(J):
                    for m, (xp, wp) in enumerate(PASSES):
                        def piece(j=j, m=m, xp=xp, wp=wp):
                            if j == 0 and m == 0 and free:
                                for s_, v_ in free:
                                    pe.wait_ge(s_, v_)
                            for c in range(C):
                                now = pe.matmul(banks[BANK_O][:, j * P:(j + 1) * P], xT[:, xp * C + c, bass.ds(b * S + j * P, P)],
                                                w_att[:, 2, wp, c, g * P:(g + 1) * P],
                                                start=m == 0 and c == 0, stop=m == 2 and c == C - 1)
                            if j == J - 1 and m == 2:
                                now.then_inc(v_summed, 1)
                        pieces.append(piece)
                return pieces

            def project_out(b, u, j, bank, free):
                pieces = []
                for c in range(C):
                    for m, (xp, wp) in enumerate(PASSES):
                        def piece(c=c, m=m, xp=xp, wp=wp):
                            if c == 0 and m == 0:
                                pe.wait_ge(o_lo, G * (b + 1))
                                for s_, v_ in free:
                                    pe.wait_ge(s_, v_)
                            now = pe.matmul(banks[bank][:], o_hl[u][:, c, xp, j * P:(j + 1) * P], w_att[:, 3, wp, c, :],
                                            start=c == 0 and m == 0, stop=c == C - 1 and m == 2)
                            if c == C - 1 and m == 2:
                                now.then_inc(wo_done, 1)
                        pieces.append(piece)
                return pieces

            def attention_step(b, u, g, prev=True, nxt=True, sums=True):
                n = G * b + g
                ahead, qk, wo, vs = two_on(b, g), [], [], []
                if ahead:
                    qk = project_qk(0, *ahead, [(qk_rotated, 2 * n + 4)]) + project_qk(1, *ahead, [(qk_rotated, 2 * n + 5)])
                if nxt:
                    vs = project_v(*((b, g + 1) if g + 1 < G else (b + 1, 0)), [(sum_done, J * (b - 1) + g + 1)] if sums else [(o_read, n)] if prev else [(v_read, 1)])
                if sums:
                    wo = project_out(b - 1, 1 - u, g, BANK_O, [(o_read, n)])
                fillers = [qk[:4], qk[4:6], qk[6:12], qk[12:18], qk[18:24], wo, vs[:3], vs[3:]]
                for done in (q_stacked, k_stacked):
                    pe.wait_ge(done[g % 2], 16 * 4 * (b * (G // 2) + g // 2 + 1))
                for k in range(UNITS):
                    if k != 2:
                        scores(b, g, k, not (isinstance(n, int) and n == 0 and k < 2))
                    for piece in fillers[k]:
                        piece()
                    if k > 0:
                        turn_p(b, g, k - 1)
                    elif prev:
                        turn_p(b, g, 7)
                    if k == 1:
                        scores(b, g, 2)
                        if prev:
                            times_v(b, g)

            pe.wait_ge(xgT_copied, NTILE)
            pe.wait_ge(w_lo_done, NM + 1)
            for g in range(2):
                for what in range(2):
                    for piece in project_qk(what, 0, g, [(qk_rotated, 2 * g + what)] if g + what else []):
                        piece()
            for piece in project_v(0, 0, []):
                piece()
            pe.wait_ge(y_scaled, NTILE)
            for g in range(G):
                attention_step(0, 0, g, prev=g > 0, sums=False)
            with pe.Fori(0, B // 2 - 1) as i:
                for u in range(2):
                    for g in range(G):
                        attention_step(fresh(pe, 2 * i + 1 + u), 1 - u, g)
            for g in range(G):
                attention_step(B - 1, 1, g, nxt=g < G - 1)
            turn_p(B, 0, 7)
            times_v(B, 0, nxt=False)
            for j in range(J):
                for piece in project_out(B - 1, 1, j, BANK_O if j % 2 == 0 else BANK_Q,
                                         [(o_read, N), (qk_rotated, 2 * N)] if j < 2 else [(sum_done, J * (B - 1) + j - 1)]):
                    piece()

        @block.vector
        def _(dve):
            own = Steps(dve, dve_own)
            own.link(dve.memset(gap[:], 0.0))
            dve.wait_ge(const_in, 16)
            own.link(dve.tensor_copy(carry[:], first_row))
            dve.wait_ge(gate_in, 16)
            dve.tensor_reduce(out=amax[:, GM:GM + 1], in_=gate_f[:], axis=AX.XY, op=ALU.max, apply_absolute_value=True).then_inc(amax_done, 1)
            dve.wait_ge(amax_everywhere, 1)
            scale_ops(dve, own, bass.ds(GM, 1)).then_inc(scale_done, 1)
            dve.wait_ge(w_hi_done, 1)
            dve.scalar_tensor_tensor(gate_hl[:, :, E:2 * E], gate_f[:], up[:, GM:GM + 1].bitcast(F32), gate_hl[:, :, 0:E],
                                     ALU.mult, ALU.subtract).then_inc(w_lo_done, 1)

            def normalise(b, u, half_b, first=False):
                dve.wait_ge(x_loaded[u], 16 * (half_b + 1))
                for j in range(J):
                    now = dve.bn_stats(stats[:, j, :], x_in[u][:, j, :])
                own.link(now, wait_apart)
                for j in range(J):
                    now = dve.bn_aggr(mean_var[:, j, :], stats[:, j, :])
                own.link(now)
                dve.tensor_scalar(var_eps[:], mean_var[:, :, 1], EPS, None, ALU.add).then_inc(var_done, 1)
                dve.wait_ge(w_loaded[u], 16 * (half_b + 1))
                dve.tensor_reduce(out=amax[:, u:u + 1], in_=w_in[u][:], axis=AX.XY, op=ALU.max, apply_absolute_value=True).then_inc(amax_done, 1)
                dve.wait_ge(std_done, b + 1)
                own.link(dve.reciprocal(r0[:], std[:]))
                own.link(dve.tensor_tensor(r1[:], r0[:], r0[:], ALU.mult))
                own.link(dve.tensor_tensor(r1[:], r1[:], var_eps[:], ALU.mult))
                own.link(dve.tensor_scalar(r1[:], r1[:], -0.5, 1.5, ALU.mult, ALU.add))
                own.link(dve.scalar_tensor_tensor(rstd[:], r0[:], float(2 ** LOG_X), r1[:], ALU.mult, ALU.mult))
                if not first:
                    dve.wait_ge(x_hi_done, b)
                    dve.wait_ge(x_lo_done, b)
                for j in range(J):
                    now = dve.tensor_scalar(x_n[:, j, :], x_in[u][:, j, :], mean_var[:, j, 0:1], rstd[:, j:j + 1],
                                            ALU.subtract, ALU.mult)
                now.then_inc(xn_done, 1)
                dve.wait_ge(amax_everywhere, b + 2)
                scale_ops(dve, own, bass.ds(b, 1), slice(u, u + 1)).then_inc(scale_done, 1)

            def low_part(b, u):
                dve.wait_ge(w_hi_done, b + 2)
                dve.scalar_tensor_tensor(w_exp[:, bass.ds(b, 1), 1, :, :].rearrange("p m c d -> p (m c d)"),
                                         w_in[u][:].rearrange("p c d -> p (c d)"), up[:, bass.ds(b, 1)].bitcast(F32),
                                         w_exp[:, bass.ds(b, 1), 0, :, :].rearrange("p m c d -> p (m c d)"),
                                         ALU.mult, ALU.subtract).then_inc(w_lo_done, 1)

            def over_e(ap):
                return ap.unsqueeze(2).broadcast_to([P, J, E])

            def route(b, u, half_b, first=False):
                dve.wait_ge(gate_done, b + 1)
                dve.tensor_reduce(out=logit[:], in_=banks[BANK_GATE + u][:, 0:2 * E * J].rearrange("p (j h e) -> p j e h", h=2, e=E),
                                  axis=AX.X, op=ALU.add).then_inc(logit_read, 1)
                dve.wait_ge(logit_read, b + 1)
                for k, of in enumerate((logit, rest)):
                    own.link(dve.tensor_reduce(out=best[:, k, :], in_=of[:], axis=AX.X, op=ALU.max))
                    own.link(dve.tensor_tensor(same[:], of[:], over_e(best[:, k, :]), ALU.is_equal))
                    own.link(dve.tensor_tensor(same[:], same[:], prefer, ALU.mult))
                    own.link(dve.tensor_reduce(out=rank[:], in_=same[:], axis=AX.X, op=ALU.max))
                    own.link(dve.tensor_tensor(one_hot[k][:], same[:], over_e(rank[:]), ALU.is_equal))
                    if k == 0:
                        own.link(dve.scalar_tensor_tensor(rest[:], one_hot[0][:], MASKED, logit[:], ALU.mult, ALU.add))
                if not first:
                    dve.wait_ge(rank_done, b)
                dve.tensor_tensor(chosen[:].rearrange("p (j e) -> p j e", j=J), one_hot[0][:], one_hot[1][:], ALU.add)\
                    .then_inc(chosen_done, 1)
                dve.tensor_tensor(gap[:, bass.ds(b * J, J)], best[:, 1, :], best[:, 0, :], ALU.subtract).then_inc(gap_done, 1)
                dve.wait_ge(rank_done, b + 1)
                own.link(dve.tensor_tensor(place_f[:], banks[BANK_RANK + u][:, 0:J * E].rearrange("p (j e) -> p j e", j=J),
                                           carry[:].unsqueeze(1).broadcast_to([P, J, E]), ALU.add))
                dve.tensor_tensor(carry[:], banks[BANK_RANK + u][:, J * E:(J + 1) * E], carry[:], ALU.add).then_inc(rank_read, 1)
                dve.wait_ge(rank_read, b + 1)
                for k in range(2):
                    own.link(dve.tensor_tensor(picked[:, k], one_hot[k][:], place_f[:], ALU.mult))
                own.link(dve.tensor_reduce(out=slot_f[:], in_=picked[:], axis=AX.X, op=ALU.add))
                here = slots[:, :, bass.ds(b * J, J)]
                own.link(dve.tensor_copy(here, slot_f[:]))
                own.link(dve.tensor_scalar(low7[:], here, P - 1, None, ALU.bitwise_and))
                own.link(dve.tensor_scalar(high[:], here, 7, None, ALU.logical_shift_right))
                if not first:
                    dve.wait_ge(scattered[u], 16 * 2 * J * half_b)
                dve.scalar_tensor_tensor(target[u][:], low7[:], float(NCOL), high[:], ALU.mult, ALU.add).then_inc(target_done, 1)

            LINKS = 2 + 5 + 3 + 11 + 1 + 2 + 1 + 3
            normalise(0, 0, 0, True)
            low_part(0, 0)
            normalise(1, 1, 0)
            route(0, 0, 0, True)
            low_part(1, 1)
            normalise(2, 0, 1)
            route(1, 1, 0, True)
            low_part(2, 0)
            own.enter(2 * LINKS)
            with dve.Fori(1, B // 2 - 1) as i:
                own.turn(i - 1)
                normalise(2 * i + 1, 1, i)
                route(2 * i, 0, i)
                low_part(2 * i + 1, 1)
                normalise(2 * i + 2, 0, i + 1)
                route(2 * i + 1, 1, i)
                low_part(2 * i + 2, 0)
            own.leave(B // 2 - 2)
            normalise(B - 1, 1, B // 2 - 1)
            route(B - 2, 0, B // 2 - 1)
            low_part(B - 1, 1)
            route(B - 1, 1, B // 2 - 1)

            for u in range(2):
                dve.wait_ge(xn_stored[u], 16 * (B // 2))
                dve.wait_ge(scattered[u], 16 * J * B)
            dve.wait_ge(xt_done, NT)
            own.link(dve.tensor_tensor(tiles[:], carry[:], first_row, ALU.subtract))
            own.link(dve.tensor_scalar(cnt_i[:], tiles[:], float(P - 1), None, ALU.add))
            own.link(dve.tensor_scalar(cnt_i[:], cnt_i[:], 7, None, ALU.logical_shift_right))
            own.link(dve.tensor_copy(tiles[:], cnt_i[:]))
            own.link(dve.tensor_copy(ends[:, 0, :], tiles[:]))
            for n in (1, 2, 4):
                a, z = (0, 1) if n != 2 else (1, 0)
                own.link(dve.tensor_copy(ends[:, z, 0:n], ends[:, a, 0:n]))
                own.link(dve.tensor_tensor(ends[:, z, n:E], ends[:, a, n:E], ends[:, a, 0:E - n], ALU.add))
            both = [P, NTILE, E]
            own.link(dve.tensor_tensor(past[:], tile_no.unsqueeze(2).broadcast_to(both), ends[:, 1, :].unsqueeze(1).broadcast_to(both),
                                       ALU.is_ge))
            own.link(dve.tensor_reduce(out=n_past[:], in_=past[:], axis=AX.X, op=ALU.add))
            own.link(dve.tensor_tensor(past[:], past[:], tiles[:].unsqueeze(1).broadcast_to(both), ALU.mult))
            own.link(dve.tensor_reduce(out=t_past[:], in_=past[:], axis=AX.X, op=ALU.add))
            own.link(dve.tensor_tensor(t_col[:], tile_no, t_past[:], ALU.subtract))
            own.link(dve.scalar_tensor_tensor(exp_col[:, 1, :], n_past[:], float(NT), t_col[:], ALU.mult, ALU.add))
            dve.tensor_scalar(exp_col[:, 0, :], n_past[:], float(E - 1), None, ALU.min).then_inc(tiles_done, 1)

            own.link(dve.tensor_tensor(moves[:], ends[:, 1, :], tiles[:], ALU.subtract))
            own.link(dve.scalar_tensor_tensor(moves[:], moves[:], float(P), first_row, ALU.mult, ALU.subtract))
            own.link(dve.tensor_scalar(slot_i[:], slots[:], (NT * P).bit_length() - 1, None, ALU.logical_shift_right))
            own.link(dve.tensor_copy(slot_e[:], slot_i[:]))
            own.link(dve.tensor_copy(slot_now[:], slots[:]))
            for e in range(E):
                own.link(dve.tensor_scalar(move[:], slot_e[:], float(e), moves[:, e:e + 1], ALU.is_equal, ALU.mult))
                own.link(dve.tensor_tensor(slot_now[:], slot_now[:], move[:], ALU.add))
            dve.tensor_copy(slots[:], slot_now[:]).then_inc(slots_final, 1)

            dve.wait_ge(gap_exp, 1)
            own.link(dve.tensor_scalar(w12[:, 0, :], w12[:, 1, :], 1.0, None, ALU.add))
            own.link(dve.reciprocal(w12[:, 0, :], w12[:, 0, :]))
            dve.tensor_tensor(w12[:, 1, :], w12[:, 1, :], w12[:, 0, :], ALU.mult).then_inc(w12_done, 1)

            def largest(m):
                dve.wait_ge(w_loaded[m % 2], 16 * (m // 2 + 1))
                dve.tensor_reduce(out=amax[:, m:m + 1], in_=wq_in[m % 2][:], axis=AX.XY, op=ALU.max, apply_absolute_value=True).then_inc(amax_done, 1)

            largest(E)
            for m in range(E, NM):
                dve.wait_ge(amax_everywhere, m + 2)
                scale_ops(dve, own, bass.ds(m, 1)).then_inc(scale_done, 1)
                if m + 1 < NM and m == E:
                    largest(m + 1)
                dve.wait_ge(w_hi_done, m + 2)
                dve.scalar_tensor_tensor(w_att[:, m - E, 1, :, :], wq_in[m % 2][:], up[:, m:m + 1].bitcast(F32),
                                         w_att[:, m - E, 0, :, :], ALU.mult, ALU.subtract).then_inc(w_lo_done, 1)
                if m + 2 < NM and m >= E:
                    largest(m + 2)

            dve.wait_ge(bias_loaded, 16)
            dve.wait_ge(w_lo_done, NM + 1)

            def scale_y(s, u, turn, first=False):
                e = dve.value_load(exp_col[0:1, 0, bass.ds(s, 1)], min_val=0, max_val=E - 1)
                dve.wait_ge(y_done, s + 1)
                if not first:
                    dve.wait_ge(y_stored[u], 16 * turn)
                dve.scalar_tensor_tensor(y_sb[u][:], banks[4 + u % 2][:], down[:, bass.ds(e, 1)].bitcast(F32),
                                         bias_all[:, bass.ds(e, 1), :].rearrange("p e d -> p (e d)"), ALU.mult, ALU.add)\
                    .then_inc(y_scaled, 1)

            for u in range(4):
                scale_y(u, u, 0, True)
            with dve.Fori(1, NTILE // 4) as i:
                for u in range(4):
                    scale_y(4 * i + u, u, i)

            q_, k_, v_, o_ = (down[:, m:m + 1].bitcast(F32) for m in range(E, NM))
            own.link(dve.tensor_tensor(factors[:, 0:1], q_, k_, ALU.mult))
            own.link(dve.tensor_scalar(factors[:, 0:1], factors[:, 0:1], 2.0 ** (2 * LOG_V) * HD ** -0.5, None, ALU.mult))
            own.link(dve.tensor_scalar(factors[:, 1:2], factors[:, 0:1], -1.0, None, ALU.mult))
            own.link(dve.tensor_tensor(factors[:, 2:3], v_, o_, ALU.mult))
            dve.tensor_scalar(factors[:, 2:3], factors[:, 2:3], 2.0 ** (LOG_V + LOG_X), None, ALU.mult).then_inc(factors_done, 1)
            for u in range(4):
                dve.wait_ge(y_stored[u], 16 * (NTILE // 4))
            dve.wait_ge(factors_done, 1)
            dve.wait_ge(trig_in, 16)

            swap = [(i + HD // 2) % HD for i in range(HD)]

            def rotate(what, n, first=False):
                w = 2 * n + what
                wait_apart(dve, qk_summed, w + 1)
                if not first:
                    wait_apart(dve, qk_lo, w - 1)
                dve.stream_shuffle(turned[what][:], banks[BANK_Q][:], swap)
                dve.tensor_tensor(plain[what][:], banks[BANK_Q][:], trig_sb[:, 0, :], ALU.mult).then_inc(qk_rotated, 1)

            def shifts(b, g, k):
                n, i = G * b + g, k // 2
                W = (i + 1) * P
                dve.wait_ge(scores_done, UNITS * n + k + 1)
                own.link(dve.tensor_reduce(out=top[:, k % 2, :], in_=s_banks(k % 2)[:, :, 0:W], axis=AX.X, op=ALU.max))
                dve.tensor_scalar(shift[:, k % 2, :], top[:, k % 2, :], factors[:, 1:2], None, ALU.mult).then_inc(shift_done, 1)

            def copy_pt(b, g, k, a):
                bank = pt_bank(g, a)
                dve.wait_ge(pt_turned, fill(G * b + g, a) + 1)
                _, view, to = part(k, a)
                dve.tensor_copy(to, view(banks[BANK_PT + bank])).then_inc(pt_copied[bank], 1)

            def reciprocals(n, g):
                dve.wait_ge(exp_done, UNITS * n)
                own.link(dve.reciprocal(rden[:, :, :, 0], den[(g - 1) % 2][:]))
                dve.tensor_copy(rden_wide[:], rden[:].broadcast_to([P, J, HG, HD])).then_inc(rden_done, 1)

            def normalise_o(b, g):
                n, bank = G * b + g, pt_bank(g, fill_r(b))
                dve.wait_ge(pv_done, n)
                dve.wait_ge(pt_copied[bank], fills_up_to(bank, b, g, fill_r(b)))
                dve.tensor_tensor(o_sb[:], banks[BANK_O][:], o_sb[:], ALU.mult).then_inc(o_read, 1)

            def add_experts(b, j):
                u, w = j % 2, J * b + j
                dve.wait_ge(x_again[u], 16 * (b * (J // 2) + j // 2 + 1))
                dve.wait_ge(y_back[u], 32 * (b * (J // 2) + j // 2 + 1))
                for k in range(2):
                    own.link(dve.scalar_tensor_tensor(sum_sb[u][:], y_in[u][:, k, :], w12[:, k, bass.ds(w, 1)], sum_sb[u][:],
                                                      ALU.mult, ALU.add))

            def add_attention(b, j, bank):
                u, w = j % 2, J * b + j
                dve.wait_ge(wo_done, w + 1)
                dve.scalar_tensor_tensor(sum_sb[u][:], banks[bank], factors[:, 2:3], sum_sb[u][:], ALU.mult, ALU.add)\
                    .then_inc(sum_done, 1)

            def attention_step(b, g, prev=True, sums=True):
                n = G * b + g
                if prev:
                    reciprocals(n, g)
                shifts(b, g, 0)
                if prev:
                    copy_pt(b, g, 7, 0)
                shifts(b, g, 1)
                shifts(b, g, 2)
                if sums:
                    add_experts(b - 1, g)
                if prev:
                    dve.wait_ge(pv_done, n)
                copy_pt(b, g, 0, fills(0, is_first(b, g))[0])
                if prev:
                    normalise_o(b, g)
                if two_on(b, g):
                    rotate(0, n + 2)
                copy_pt(b, g, 1, 4)
                shifts(b, g, 3)
                copy_pt(b, g, 2, 5)
                for k, a in ((4, None), (5, 7), (6, 9), (7, 11)):
                    shifts(b, g, k)
                    if k == 4 and two_on(b, g):
                        rotate(1, n + 2)
                    if a:
                        copy_pt(b, g, k - 1, a)
                    if k == 5 and sums:
                        add_attention(b - 1, g, BANK_O)

            for n in range(2):
                for what in range(2):
                    rotate(what, n, n == 0)
            for g in range(G):
                attention_step(0, g, prev=g > 0, sums=False)
            own.enter(2 * (G * (UNITS + 1) + 2 * J))
            with dve.Fori(0, B // 2 - 1) as i:
                own.turn(i)
                for b in (2 * i + 1, 2 * i + 2):
                    for g in range(G):
                        attention_step(b, g)
            own.leave(B // 2 - 1)
            for g in range(G):
                attention_step(B - 1, g)
            reciprocals(N, 0)
            copy_pt(B, 0, 7, 0)
            normalise_o(B, 0)
            for j in range(J):
                add_experts(B - 1, j)
                add_attention(B - 1, j, BANK_O if j % 2 == 0 else BANK_Q)


def kernel(**inputs):
    from concourse import bacc
    from concourse.bass_utils import run_bass_kernel_spmd

    a = {k: np.asarray(v) for k, v in inputs.items()}
    x = a["L0_attn_x"]
    B, S, D = x.shape
    E = a["L0_ffn_gate_w"].shape[0]
    J, C, T = S // P, D // P, B * S
    NTILE = -(-(2 * (T // P) + E - 1) // 4) * 4

    def chunks(w):
        return w.T.reshape(C, P, w.shape[0]).transpose(1, 0, 2)

    mats = [a["L0_ffn_expert_w"][e] for e in range(E)] + [a["L0_attn_" + n] for n in ("Wq", "Wk", "Wv", "Wo")]
    HEAD = D // 16
    inv_freq = (np.float32(1.0) / np.power(np.float32(10000.0), np.arange(0, HEAD, 2, dtype=np.float32) / np.float32(HEAD))).astype(np.float32)
    freqs = np.outer(np.arange(S, dtype=np.float32), inv_freq).astype(np.float32)
    emb = np.concatenate([freqs, freqs], axis=-1).T
    sign = np.where(np.arange(HEAD) < HEAD // 2, -1.0, 1.0)[:, None]
    down = 2.0 ** -LOG_V
    trig = np.stack([np.tile(np.cos(emb) * down, (4, 1)), np.tile(np.sin(emb) * sign * down, (4, 1))], axis=1).astype(np.float32)
    small = np.concatenate([np.tile(E - np.arange(E), J), np.arange(E) * T, np.arange(NTILE)]).astype(np.float32)
    arrays = {
        "x": x,
        "w_all": np.ascontiguousarray(np.stack([chunks(w) for w in mats])),
        "gate": np.ascontiguousarray(chunks(a["L0_ffn_gate_w"])),
        "bias": a["L0_ffn_expert_b"],
        "trig": trig,
        "small": np.tile(small, (P, 1)),
    }
    nc = bacc.Bacc("TRN2", target_bir_lowering=False, num_devices=1)
    args = [nc.dram_tensor(n, v.shape, mybir.dt.from_np(v.dtype), kind="ExternalInput").ap() for n, v in arrays.items()]
    out = nc.dram_tensor("out", x.shape, F32, kind="ExternalOutput").ap()
    moe_attention_layer(nc, *args, out)
    r = run_bass_kernel_spmd(nc, [arrays], core_ids=[0])
    return r.results[0]["out"]
```
